# Optimizing a Trainium2 kernel written in Bass

```python
import numpy as np
import jax
import jax.numpy as jnp

def _softmax(x, axis=-1):
    return jax.nn.softmax(x, axis=axis)

def _gelu(x):
    return jax.nn.gelu(x, approximate=True)

def _silu(x):
    return jax.nn.silu(x)

def _sigmoid(x):
    return jax.nn.sigmoid(x)

def _layernorm(x, axis=-1, eps=1e-05):
    m = jnp.mean(x, axis=axis, keepdims=True)
    v = jnp.var(x, axis=axis, keepdims=True)
    return (x - m) / jnp.sqrt(v + eps)

def _scatter_add(tgt, idx, src, axis=0):
    return tgt.at[idx].add(src)

def _segment_sum(src, seg, n):
    return jax.ops.segment_sum(src, seg, n)
kernel_name = 'mk_prb_d1_jaxref_r4_488456'

def setup_inputs(seed: int=0):
    np.random.seed(seed)
    _w = jnp.asarray

    def _L0_attn_setup():
        import jax, jax.numpy as jnp
        import numpy as np
        B, L, D = (4, 1024, 256)
        LN_EPS = 1e-05
        SCAN_EPS = 1e-08
        key = jax.random.key(seed)
        ks = jax.random.split(key, 5)
        s = 1.0 / np.sqrt(D)
        return {'X': jax.random.normal(ks[0], (B, L, D), dtype=jnp.float32), 'Wa': jax.random.normal(ks[1], (D, D), dtype=jnp.float32) * s, 'ba': jnp.zeros((D,), dtype=jnp.float32), 'Wb': jax.random.normal(ks[2], (D, D), dtype=jnp.float32) * s, 'bb': jnp.zeros((D,), dtype=jnp.float32), 'Wc': jax.random.normal(ks[3], (D, D), dtype=jnp.float32) * s, 'bc': jnp.zeros((D,), dtype=jnp.float32), 'gamma': jnp.ones((D,), dtype=jnp.float32), 'beta': jnp.zeros((D,), dtype=jnp.float32), 'h0': jax.random.normal(ks[4], (1, D), dtype=jnp.float32)}
    _L0_attn_in = _L0_attn_setup()

    def _L0_ffn_setup():
        import jax, jax.numpy as jnp
        import numpy as np
        EMB = 256
        FF = 4 * EMB

        def _ternary(w):
            scale = jnp.maximum(jnp.mean(jnp.abs(w)), 1e-08)
            w_t = jnp.clip(jnp.round(w / scale), -1.0, 1.0)
            return w + jax.lax.stop_gradient(w_t - w)
        key = jax.random.key(seed)
        kx, k1, k2, kb1, kb2 = jax.random.split(key, 5)
        x = jax.random.normal(kx, (4, 512, EMB), dtype=jnp.float32)
        lim1 = 1.0 / np.sqrt(EMB)
        lim2 = 1.0 / np.sqrt(FF)
        W1 = jax.random.uniform(k1, (FF, EMB), jnp.float32, -lim1, lim1)
        b1 = jax.random.uniform(kb1, (FF,), jnp.float32, -lim1, lim1)
        W2 = jax.random.uniform(k2, (EMB, FF), jnp.float32, -lim2, lim2)
        b2 = jax.random.uniform(kb2, (EMB,), jnp.float32, -lim2, lim2)
        return {'x': x, 'W1': W1, 'b1': b1, 'W2': W2, 'b2': b2}
    _L0_ffn_in = _L0_ffn_setup()
    _d = {'L0_attn_X': _L0_attn_in['X'], 'L0_attn_Wa': _L0_attn_in['Wa'], 'L0_attn_ba': _L0_attn_in['ba'], 'L0_attn_Wb': _L0_attn_in['Wb'], 'L0_attn_bb': _L0_attn_in['bb'], 'L0_attn_Wc': _L0_attn_in['Wc'], 'L0_attn_bc': _L0_attn_in['bc'], 'L0_attn_gamma': _L0_attn_in['gamma'], 'L0_attn_beta': _L0_attn_in['beta'], 'L0_attn_h0': _L0_attn_in['h0'], 'L0_ffn_W1': _L0_ffn_in['W1'], 'L0_ffn_b1': _L0_ffn_in['b1'], 'L0_ffn_W2': _L0_ffn_in['W2'], 'L0_ffn_b2': _L0_ffn_in['b2']}
    _x0 = _d['L0_attn_X']
    _d['L0_attn_X'] = jax.random.normal(jax.random.fold_in(jax.random.key(seed), 1), (4, 1024, 256), dtype=_x0.dtype)
    del _x0
    return _d

def reference(L0_attn_X, L0_attn_Wa, L0_attn_ba, L0_attn_Wb, L0_attn_bb, L0_attn_Wc, L0_attn_bc, L0_attn_gamma, L0_attn_beta, L0_attn_h0, L0_ffn_W1, L0_ffn_b1, L0_ffn_W2, L0_ffn_b2):

    def _L0_attn_ref(X, Wa, ba, Wb, bb, Wc, bc, gamma, beta, h0):
        import jax, jax.numpy as jnp
        import numpy as np
        B, L, D = (4, 1024, 256)
        LN_EPS = 1e-05
        SCAN_EPS = 1e-08
        mu = jnp.mean(X, axis=-1, keepdims=True)
        var = jnp.mean(jnp.square(X - mu), axis=-1, keepdims=True)
        Z = (X - mu) * jax.lax.rsqrt(var + LN_EPS) * gamma + beta
        A = jax.nn.sigmoid(jnp.einsum('bld,ed->ble', Z, Wa) + ba)
        P = jnp.cumprod(A, axis=1)
        Bx = jnp.einsum('bld,ed->ble', Z, Wb) + bb
        S = jnp.cumsum(Bx / (P + SCAN_EPS), axis=1)
        h = P * (h0[:, None, :] + S)
        C = jnp.einsum('bld,ed->ble', Z, Wc) + bc
        return C * h + X

    def _L0_ffn_ref(x, W1, b1, W2, b2):
        import jax, jax.numpy as jnp
        import numpy as np
        EMB = 256
        FF = 4 * EMB

        def _ternary(w):
            scale = jnp.maximum(jnp.mean(jnp.abs(w)), 1e-08)
            w_t = jnp.clip(jnp.round(w / scale), -1.0, 1.0)
            return w + jax.lax.stop_gradient(w_t - w)
        h = jnp.einsum('bsd,fd->bsf', x, _ternary(W1)) + b1
        h = jax.nn.gelu(h, approximate=False)
        out = jnp.einsum('bsf,df->bsd', h, _ternary(W2)) + b2
        return out
    x = L0_attn_X
    xn = _layernorm(x, axis=-1)
    x = x + _L0_attn_ref(xn, L0_attn_Wa, L0_attn_ba, L0_attn_Wb, L0_attn_bb, L0_attn_Wc, L0_attn_bc, L0_attn_gamma, L0_attn_beta, L0_attn_h0) + _L0_ffn_ref(xn, L0_ffn_W1, L0_ffn_b1, L0_ffn_W2, L0_ffn_b2)
    return x

_drawn_inputs = setup_inputs


def setup_inputs(seed=0):
    import zlib

    import numpy as np

    out = dict(_drawn_inputs(seed))
    spreads = {'L0_attn_ba': (0.0, 0.8),
     'L0_attn_bb': (0.0, 2.0),
     'L0_attn_bc': (0.0, 2.0),
     'L0_attn_gamma': (1.0, 0.6),
     'L0_attn_beta': (0.0, 0.8)}
    factors = {'L0_attn_Wa': 8.0,
     'L0_attn_Wb': 8.0,
     'L0_attn_Wc': 8.0,
     'L0_attn_h0': 39.373,
     'L0_ffn_b1': 24.272,
     'L0_ffn_b2': 64.0}
    for name, (base, spread) in spreads.items():
        noise = np.random.default_rng([zlib.crc32(name.encode()), seed]).standard_normal(out[name].shape)
        drawn = base * np.exp(spread * noise) if base else spread * noise
        out[name] = jnp.asarray(drawn.astype(out[name].dtype))
    for name, factor in factors.items():
        out[name] = (out[name] * factor).astype(out[name].dtype)
    return out
```

```python
from contextlib import ExitStack

import concourse.bass as bass
from concourse import mybir

P = 128
ALU = mybir.AluOpType
ACT = mybir.ActivationFunctionType
F32 = mybir.dt.float32
F16 = mybir.dt.float16

LN_EPS = 1e-5
SCAN_EPS = 1e-8
TERNARY_EPS = 1e-8

ROW_SCALE = 2.0**10
WEIGHT_SCALE = 2.0**6
PROJ_SCALE = ROW_SCALE * WEIGHT_SCALE
G_BUFFERS = 4


def build(nc, X, Wa, ba, Wb, bb, Wc, bc, gamma, beta, h0, W1, b1, W2, b2, out):
    TILES, L, D = X.shape
    FF = W1.shape[0]
    SUBS = L // P
    KB = D // P
    FB = FF // P
    HALF = L // 2
    NPROJ = 3 * KB
    BN = 6
    assert L == 1024 and KB == 2 and FB == 8 and TILES >= 3

    PROJ_BIAS, GAMMA, BETA, STATE0, B2 = 0, NPROJ, NPROJ + KB, NPROJ + 2 * KB, NPROJ + 3 * KB
    B1 = NPROJ + 4 * KB
    NPAR = B1 + FB

    x_rows = X.rearrange("b (s p) d -> p b s d", p=P)
    out_rows = out.rearrange("b (s p) d -> p b s d", p=P)

    with ExitStack() as ctx:

        def sb(name, shape, dt=F32):
            return ctx.enter_context(nc.sbuf_tensor(name, shape, dt))

        def sem(name):
            return ctx.enter_context(nc.semaphore(name))

        slot = [ctx.enter_context(nc.psum_tensor(f"slot{i}", [P, L], F32)) for i in range(4)]

        rows = sb("rows", [P, TILES * SUBS * D])
        xn = sb("xn", [P, SUBS, D])
        zn = sb("zn", [P, SUBS, D])
        x_hi = sb("x_hi", [P, KB, L], F16)
        x_lo = sb("x_lo", [P, KB, L], F16)
        z_hi = sb("z_hi", [P, KB, L], F16)
        z_lo = sb("z_lo", [P, KB, L], F16)
        decay = sb("decay", [P, KB, L])
        inverse = sb("inverse", [P, KB, L])
        state = sb("state", [P, KB, L])
        zeros = sb("zeros", [P, L])
        gelu = sb("gelu", [P, G_BUFFERS, L])
        g_hi = sb("g_hi", [P, FB, L], F16)
        g_lo = sb("g_lo", [P, FB, L], F16)
        bn = sb("bn", [P, SUBS, BN])
        halves = sb("halves", [P, 4, SUBS])
        mean_sum, mean_gap, square_sum, gap_square = (halves[:, i, :] for i in range(4))
        mean = sb("mean", [P, SUBS])
        var = sb("var", [P, SUBS])
        eps_column = sb("eps_column", [P, SUBS])
        scalars = sb("scalars", [P, 5, SUBS])
        var_eps, rstd, var_n, var_n_eps, rstd_n = (scalars[:, i, :] for i in range(5))
        minus_half = sb("minus_half", [P, SUBS])

        ident = sb("ident", [P, P])
        ident16 = sb("ident16", [P, P], F16)
        averager = sb("averager", [P, P])
        par_rows = sb("par_rows", [NPAR, P])
        par = sb("par", [P, NPAR])
        bias_proj = sb("bias_proj", [P, NPROJ])
        bias_scaled = sb("bias_scaled", [P, NPROJ])
        gamma_scaled = sb("gamma_scaled", [P, KB])
        state0_scaled = sb("state0_scaled", [P, KB])
        w_proj = sb("w_proj", [P, NPROJ, D])
        wT_raw = sb("wT_raw", [P, KB, NPROJ * P])
        wT_scaled = sb("wT_scaled", [P, KB, NPROJ * P])
        w_hi = sb("w_hi", [P, KB, NPROJ * P], F16)
        w_lo = sb("w_lo", [P, KB, NPROJ * P], F16)
        w1_rows = g_hi[:, 0:4, :].rearrange("p a b -> p (a b)").bitcast(F32)
        w2_rows = g_hi[:, 4:8, :].rearrange("p a b -> p (a b)").bitcast(F32)
        w1_tern = g_lo[:, 0:2, :].rearrange("p a b -> p (a b)")
        w2_tern = g_lo[:, 2:4, :].rearrange("p a b -> p (a b)")
        negatives = g_lo[:, 4:8, :].rearrange("p (m a) b -> p m (a b)", m=2)
        magnitudes = gelu[:, 0:2, :].rearrange("p a b -> p (a b)")
        abs_sums = sb("abs_sums", [P, 2])
        threshold = sb("threshold", [P, 2])
        minus_threshold = sb("minus_threshold", [P, 2])
        w1T = sb("w1T", [P, KB, FF], F16)
        w2T = sb("w2T", [P, FB, D], F16)

        x_loaded = sem("x_loaded")
        par_loaded = sem("par_loaded")
        proj_loaded = sem("proj_loaded")
        w1_loaded = sem("w1_loaded")
        w2_loaded = sem("w2_loaded")
        out_stored = sem("out_stored")
        pool_consts = sem("pool_consts")
        ident_started = sem("ident_started")
        ident_made = sem("ident_made")
        ident16_made = sem("ident16_made")
        par_turned = sem("par_turned")
        par_ready = sem("par_ready")
        par_scaled = sem("par_scaled")
        proj_turned = sem("proj_turned")
        proj_scaled = sem("proj_scaled")
        proj_raw = sem("proj_raw")
        proj_hi = sem("proj_hi")
        proj_lo = sem("proj_lo")
        beta_applied = sem("beta_applied")
        bias_summed = sem("bias_summed")
        bias_ready = sem("bias_ready")
        abs_summed = sem("abs_summed")
        mean_abs = sem("mean_abs")
        mean_floored = sem("mean_floored")
        threshold_ready = sem("threshold_ready")
        negatives_ready = sem("negatives_ready")
        ternary_ready = sem("ternary_ready")
        ternary_turned = sem("ternary_turned")
        ternary_placed = sem("ternary_placed")
        bn_done = sem("bn_done")
        halves_done = sem("halves_done")
        moments_done = sem("moments_done")
        scalars_done = sem("scalars_done")
        xn_done = sem("xn_done")
        zn_done = sem("zn_done")
        residual_done = sem("residual_done")
        z_turned = sem("z_turned")
        x_turned = sem("x_turned")
        z_hi_done = sem("z_hi_done")
        z_lo_done = sem("z_lo_done")
        x_hi_done = sem("x_hi_done")
        x_lo_done = sem("x_lo_done")
        gate_summed = sem("gate_summed")
        gate_done = sem("gate_done")
        in_summed = sem("in_summed")
        read_summed = sem("read_summed")
        decay_done = sem("decay_done")
        shifted_done = sem("shifted_done")
        inverse_done = sem("inverse_done")
        term_done = sem("term_done")
        sum_done = sem("sum_done")
        state_done = sem("state_done")
        read_done = sem("read_done")
        up_summed = sem("up_summed")
        gelu_done = sem("gelu_done")
        g_hi_done = sem("g_hi_done")
        g_lo_done = sem("g_lo_done")
        down_summed = sem("down_summed")
        mixed_done = sem("mixed_done")
        out_turned = sem("out_turned")
        out_done = sem("out_done")

        block = ctx.enter_context(nc.Block())

        def tile_rows(t, first, n):
            return rows[:, bass.ds(t * (SUBS * D) + first * D, n * D)]

        @block.sync
        def _(sp):
            for t in range(TILES):
                if t > 0:
                    sp.wait_ge(x_loaded, 16 * t)
                sp.dma_start(tile_rows(t, 0, SUBS).rearrange("p (s d) -> p s d", d=D),
                             x_rows[:, t]).then_inc(x_loaded, 16)
            with sp.Fori(0, TILES) as t:
                for half in range(2):
                    sp.wait_ge(out_done, t * 2 + half + 1)
                    n = SUBS // 2
                    sp.dma_start(out_rows[:, bass.ds(t, 1), half * n:(half + 1) * n, :],
                                 tile_rows(t, half * n, n).rearrange("p (b s d) -> p b s d", b=1, d=D)
                                 ).then_inc(out_stored, 16)
            sp.wait_ge(out_stored, 16 * 2 * TILES)

        @block.gpsimd
        def _(pool):
            nc.gpsimd.memset(ident[:], 0.0).then_inc(ident_started, 1)
            pool.wait_ge(ident_started, 1)
            nc.gpsimd.affine_select(out=ident[:], in_=ident[:], compare_op=ALU.not_equal, fill=1.0,
                                    base=0, pattern=[[-1, P]], channel_multiplier=1).then_inc(ident_made, 1)
            nc.gpsimd.memset(minus_half[:], -0.5).then_inc(pool_consts, 1)
            nc.gpsimd.memset(eps_column[:], LN_EPS).then_inc(pool_consts, 1)
            nc.gpsimd.memset(averager[:], 1.0 / (FF * D)).then_inc(pool_consts, 1)
            nc.gpsimd.memset(zeros[:], 0.0).then_inc(pool_consts, 1)

            def norm_scalars(t):
                n = 6 * t
                pool.wait_ge(moments_done, 2 * t + 2)
                nc.gpsimd.tensor_tensor(var_eps, var[:], eps_column[:], ALU.add).then_inc(scalars_done, 1)
                pool.wait_ge(scalars_done, n + 1)
                nc.gpsimd.tensor_tensor(rstd, var_eps, minus_half[:], ALU.pow).then_inc(scalars_done, 1)
                pool.wait_ge(scalars_done, n + 2)
                nc.gpsimd.tensor_tensor(var_n, var[:], rstd, ALU.mult).then_inc(scalars_done, 1)
                pool.wait_ge(scalars_done, n + 3)
                nc.gpsimd.tensor_tensor(var_n_eps, var_n, rstd, ALU.mult).then_inc(scalars_done, 1)
                pool.wait_ge(scalars_done, n + 4)
                nc.gpsimd.tensor_tensor(var_n, var_n_eps, eps_column[:], ALU.add).then_inc(scalars_done, 1)
                pool.wait_ge(scalars_done, n + 5)
                nc.gpsimd.tensor_tensor(rstd_n, var_n, minus_half[:], ALU.pow).then_inc(scalars_done, 1)

            def residuals(t):
                for half in range(2):
                    n = SUBS // 2
                    pool.wait_ge(xn_done, SUBS * t + n * (half + 1))
                    r = tile_rows(t, half * n, n)
                    nc.gpsimd.tensor_tensor(r, r, xn[:, half * n:(half + 1) * n, :].rearrange("p s d -> p (s d)"),
                                            ALU.add).then_inc(residual_done, 1)

            def tile(t, last):
                if not last:
                    norm_scalars(t + 1)
                for f in range(FB):
                    pool.wait_ge(g_hi_done, FB * t + f + 1)
                    nc.gpsimd.tensor_tensor(g_lo[:, f, :], gelu[:, f % G_BUFFERS, :], g_hi[:, f, :],
                                            ALU.subtract).then_inc(g_lo_done, 1)
                if not last:
                    residuals(t + 1)

            pool.wait_ge(pool_consts, 2)
            norm_scalars(0)
            residuals(0)
            tile(0, False)
            with pool.Fori(1, TILES - 1) as t:
                tile(t, False)
            tile(TILES - 1, True)

        @block.scalar
        def _(act):
            for at, v in ((PROJ_BIAS, ba), (PROJ_BIAS + KB, bb), (PROJ_BIAS + 2 * KB, bc), (GAMMA, gamma),
                          (BETA, beta), (STATE0, h0.rearrange("a d -> (a d)")), (B2, b2), (B1, b1)):
                n = v.shape[0] // P
                act.dma_start(par_rows[at:at + n, :], v.rearrange("(k p) -> k p", p=P)).then_inc(par_loaded, 16)
            for i, w in enumerate((Wa, Wb, Wc)):
                act.dma_start(w_proj[:, i * KB:(i + 1) * KB, :],
                              w.rearrange("(k p) d -> p k d", p=P)).then_inc(proj_loaded, 16)
            act.dma_start(w1_rows.rearrange("p (f d) -> p f d", d=D),
                          W1.rearrange("(f p) d -> p f d", p=P)).then_inc(w1_loaded, 16)
            act.dma_start(w2_rows.rearrange("p (k f) -> p k f", f=FF),
                          W2.rearrange("(k p) f -> p k f", p=P)).then_inc(w2_loaded, 16)

            act.wait_ge(ident_made, 1)
            nc.scalar.copy(ident16[:], ident[:]).then_inc(ident16_made, 1)

            def second_norm(t):
                act.wait_ge(scalars_done, 6 * t + 6)
                for s in range(SUBS):
                    act.wait_ge(xn_done, SUBS * t + s + 1)
                    nc.scalar.mul(zn[:, s, :], xn[:, s, :], rstd_n[:, s:s + 1]).then_inc(zn_done, 1)

            def high_part(t, k, turned, hi, done):
                act.wait_ge(turned, KB * t + k + 1)
                nc.scalar.activation(hi[:, k, :], slot[2 + k][:], ACT.Copy, scale=ROW_SCALE).then_inc(done, 1)

            second_norm(0)
            for k in range(KB):
                act.wait_ge(proj_scaled, k + 1)
                nc.scalar.copy(wT_raw[:, k, :], slot[k][:, 0:NPROJ * P]).then_inc(proj_raw, 1)
                nc.scalar.copy(w_hi[:, k, :], wT_scaled[:, k, :]).then_inc(proj_hi, 1)
            for k in range(KB):
                high_part(0, k, z_turned, z_hi, z_hi_done)
            for m, (w, loaded) in enumerate(((w1_rows, w1_loaded), (w2_rows, w2_loaded))):
                act.wait_ge(loaded, 16)
                if m:
                    act.wait_ge(abs_summed, m)
                nc.scalar.activation(magnitudes, w, ACT.Abs, accum_out=abs_sums[:, m:m + 1]).then_inc(abs_summed, 1)
            for k in range(KB):
                high_part(0, k, x_turned, x_hi, x_hi_done)

            def tile(t, last):
                for e in range(KB):
                    act.wait_ge(gate_summed, KB * t + e + 1)
                    nc.scalar.activation(decay[:, e, :], slot[2 + e][:], ACT.Sigmoid, bias=bias_proj[:, e:e + 1],
                                         scale=1.0 / PROJ_SCALE).then_inc(gate_done, 1)

                def g_high(f):
                    act.wait_ge(gelu_done, FB * t + f + 1)
                    nc.scalar.copy(g_hi[:, f, :], gelu[:, f % G_BUFFERS, :]).then_inc(g_hi_done, 1)

                for f in range(FB):
                    act.wait_ge(up_summed, FB * t + f + 1)
                    if f >= G_BUFFERS:
                        act.wait_ge(g_lo_done, FB * t + f - G_BUFFERS + 1)
                    nc.scalar.activation(gelu[:, f % G_BUFFERS, :], slot[(2 + f) % 4][:], ACT.Gelu,
                                         bias=par[:, B1 + f:B1 + f + 1], scale=1.0 / ROW_SCALE).then_inc(gelu_done, 1)
                    if f >= 1:
                        g_high(f - 1)
                g_high(FB - 1)
                if not last:
                    second_norm(t + 1)
                    for k in range(KB):
                        high_part(t + 1, k, z_turned, z_hi, z_hi_done)
                    for k in range(KB):
                        high_part(t + 1, k, x_turned, x_hi, x_hi_done)

            act.wait_ge(bias_ready, 1)
            tile(0, False)
            with act.Fori(1, TILES - 1) as t:
                tile(t, False)
            tile(TILES - 1, True)

        @block.tensor
        def _(pe):
            def turn_norm(t, k, src, produced, turned):
                if produced is not None:
                    pe.wait_ge(produced, SUBS * t + SUBS)
                for s in range(SUBS):
                    mm = nc.tensor.transpose(slot[2 + k][:, s * P:(s + 1) * P], src[:, s, k * P:(k + 1) * P], ident[:])
                mm.then_inc(turned, 1)

            def project(dst, j, summed):
                passes = [(w, z, k) for w, z in ((w_hi, z_hi), (w_hi, z_lo), (w_lo, z_hi)) for k in range(KB)]
                for n, (w, z, k) in enumerate(passes):
                    for half in range(2):
                        c = slice(half * HALF, (half + 1) * HALF)
                        mm = nc.tensor.matmul(dst[:, c], w[:, k, j * P:(j + 1) * P], z[:, k, c],
                                              start=(n == 0), stop=(n == len(passes) - 1))
                mm.then_inc(summed, 1)

            pe.wait_ge(ident_made, 1)
            pe.wait_ge(par_loaded, 16 * 8)
            nc.tensor.transpose(slot[0][:, 0:NPAR], par_rows[:], ident[0:NPAR, 0:NPAR]).then_inc(par_turned, 1)
            pe.wait_ge(proj_loaded, 16 * 3)
            pe.wait_ge(par_ready, 1)
            for k in range(KB):
                for j in range(NPROJ):
                    mm = nc.tensor.transpose(slot[k][:, j * P:(j + 1) * P], w_proj[:, j, k * P:(k + 1) * P], ident[:])
                mm.then_inc(proj_turned, 1)
            for k in range(KB):
                turn_norm(0, k, zn, zn_done, z_turned)
            pe.wait_ge(proj_raw, KB)
            for j in range(NPROJ):
                for k in range(KB):
                    mm = nc.tensor.matmul(slot[0][:, j:j + 1], wT_raw[:, k, j * P:(j + 1) * P],
                                          par[:, BETA + k:BETA + k + 1], start=(k == 0), stop=(k == KB - 1))
            mm.then_inc(beta_applied, 1)
            pe.wait_ge(pool_consts, 3)
            pe.wait_ge(abs_summed, 2)
            nc.tensor.matmul(slot[1][:, 0:2], averager[:], abs_sums[:], start=True, stop=True).then_inc(mean_abs, 1)
            for k in range(KB):
                pe.wait_ge(z_lo_done, k + 1)
                turn_norm(0, k, xn, None, x_turned)
            pe.wait_ge(ident16_made, 1)
            pe.wait_ge(bias_summed, 1)
            pe.wait_ge(ternary_ready, 1)
            w1_out, w2_out = slot[0][:].bitcast(F16), slot[1][:].bitcast(F16)
            for k in range(KB):
                for f in range(FB):
                    mm = nc.tensor.transpose(w1_out[:, k * FF + f * P:k * FF + (f + 1) * P],
                                             w1_tern[:, f * D + k * P:f * D + (k + 1) * P], ident16[:])
            mm.then_inc(ternary_turned, 1)
            pe.wait_ge(ternary_ready, 2)
            for f in range(FB):
                for k in range(KB):
                    mm = nc.tensor.transpose(w2_out[:, f * D + k * P:f * D + (k + 1) * P],
                                             w2_tern[:, k * FF + f * P:k * FF + (f + 1) * P], ident16[:])
            mm.then_inc(ternary_turned, 1)
            pe.wait_ge(proj_lo, KB)

            def turn_out(t, half):
                pe.wait_ge(mixed_done, KB * t + KB)
                for s in range(SUBS // 2):
                    for e in range(KB):
                        tok = (half * (SUBS // 2) + s) * P
                        mm = nc.tensor.transpose(slot[half][:, s * D + e * P:s * D + (e + 1) * P],
                                                 state[:, e, tok:tok + P], ident[:])
                mm.then_inc(out_turned, 1)

            def down(t, k):
                for f in range(FB):
                    pe.wait_ge(g_lo_done, FB * t + f + 1)
                    for g in (g_hi, g_lo):
                        for half in range(2):
                            c = slice(half * HALF, (half + 1) * HALF)
                            mm = nc.tensor.matmul(slot[k][:, c], w2T[:, f, k * P:(k + 1) * P], g[:, f, c],
                                                  start=(f == 0 and g is g_hi), stop=(f == FB - 1 and g is g_lo))
                mm.then_inc(down_summed, 1)

            def tile(t, first, last):
                for e in range(KB):
                    pe.wait_ge(z_lo_done, KB * t + KB)
                    pe.wait_ge(x_lo_done, KB * t + e + 1)
                    project(slot[2 + e], e, gate_summed)
                if not first:
                    for half in range(2):
                        turn_out(t - 1, half)
                else:
                    pe.wait_ge(ternary_placed, 2)
                pe.wait_ge(x_lo_done, KB * t + KB)
                for f in range(FB):
                    if f < 2:
                        pe.wait_ge(gate_done, KB * t + f + 1)
                    elif f < 4:
                        if not first:
                            pe.wait_ge(out_done, 2 * t - 2 + (f - 2) + 1)
                    else:
                        pe.wait_ge(gelu_done, FB * t + f - 4 + 1)
                    dst = slot[(2 + f) % 4]
                    for k in range(KB):
                        for n, xs in enumerate((x_hi, x_lo)):
                            for half in range(2):
                                c = slice(half * HALF, (half + 1) * HALF)
                                mm = nc.tensor.matmul(dst[:, c], w1T[:, k, f * P:(f + 1) * P], xs[:, k, c],
                                                      start=(k == 0 and n == 0), stop=(k == KB - 1 and n == 1))
                    mm.then_inc(up_summed, 1)
                for e in range(KB):
                    pe.wait_ge(gelu_done, FB * t + 5 + 2 * e)
                    project(slot[2 - 2 * e], KB + e, in_summed)
                    pe.wait_ge(gelu_done, FB * t + 6 + 2 * e)
                    project(slot[3 - 2 * e], 2 * KB + e, read_summed)
                if not last:
                    pe.wait_ge(term_done, KB * t + 1)
                    turn_norm(t + 1, 0, zn, zn_done, z_turned)
                    pe.wait_ge(read_done, KB * t + 1)
                    turn_norm(t + 1, 1, zn, zn_done, z_turned)
                pe.wait_ge(term_done, KB * t + 2)
                down(t, 0)
                if not last:
                    for k in range(KB):
                        pe.wait_ge(z_lo_done, KB * t + KB + k + 1)
                        turn_norm(t + 1, k, xn, None, x_turned)
                pe.wait_ge(read_done, KB * t + 2)
                down(t, 1)

            tile(0, True, False)
            with pe.Fori(1, TILES - 1) as t:
                tile(t, False, False)
            tile(TILES - 1, False, True)
            for half in range(2):
                turn_out(TILES - 1, half)

        @block.vector
        def _(dve):
            def statistics(t):
                dve.wait_ge(x_loaded, 16 * t + 16)
                for s in range(SUBS):
                    nc.vector.bn_stats(bn[:, s, :], tile_rows(t, s, 1)).then_inc(bn_done, 1)
                n = 4 * t
                dve.wait_ge(bn_done, SUBS * t + SUBS)
                nc.vector.tensor_tensor(mean_gap, bn[:, :, 1], bn[:, :, 4], ALU.subtract).then_inc(halves_done, 1)
                nc.vector.tensor_tensor(mean_sum, bn[:, :, 1], bn[:, :, 4], ALU.add).then_inc(halves_done, 1)
                nc.vector.tensor_tensor(square_sum, bn[:, :, 2], bn[:, :, 5], ALU.add).then_inc(halves_done, 1)
                dve.wait_ge(halves_done, n + 1)
                nc.vector.scalar_tensor_tensor(gap_square, mean_gap, 0.25, mean_gap,
                                               ALU.mult, ALU.mult).then_inc(halves_done, 1)
                dve.wait_ge(halves_done, n + 2)
                nc.vector.tensor_scalar(mean[:], mean_sum, 0.5, None, ALU.mult).then_inc(moments_done, 1)
                dve.wait_ge(halves_done, n + 4)
                nc.vector.scalar_tensor_tensor(var[:], square_sum, 1.0 / D, gap_square,
                                               ALU.mult, ALU.add).then_inc(moments_done, 1)

            def first_norm(t):
                dve.wait_ge(scalars_done, 6 * t + 2)
                for s in range(SUBS):
                    nc.vector.tensor_scalar(xn[:, s, :], tile_rows(t, s, 1), mean[:, s:s + 1], rstd[:, s:s + 1],
                                            ALU.subtract, ALU.mult).then_inc(xn_done, 1)

            def low_part(t, k, hi_done, hi, lo, done):
                dve.wait_ge(hi_done, KB * t + k + 1)
                nc.vector.scalar_tensor_tensor(lo[:, k, :], slot[2 + k][:], ROW_SCALE, hi[:, k, :],
                                               ALU.mult, ALU.subtract).then_inc(done, 1)

            statistics(0)
            dve.wait_ge(par_turned, 1)
            nc.vector.tensor_copy(par[:], slot[0][:, 0:NPAR]).then_inc(par_ready, 1)
            dve.wait_ge(par_ready, 1)
            nc.vector.tensor_scalar(gamma_scaled[:], par[:, GAMMA:GAMMA + KB], WEIGHT_SCALE, None,
                                    ALU.mult).then_inc(par_scaled, 1)
            nc.vector.tensor_scalar(state0_scaled[:], par[:, STATE0:STATE0 + KB], 1.0 / PROJ_SCALE, None,
                                    ALU.mult).then_inc(par_scaled, 1)
            first_norm(0)
            dve.wait_ge(par_scaled, 1)
            for k in range(KB):
                dve.wait_ge(proj_turned, k + 1)
                nc.vector.tensor_scalar(wT_scaled[:, k, :], slot[k][:, 0:NPROJ * P], gamma_scaled[:, k:k + 1], None,
                                        ALU.mult).then_inc(proj_scaled, 1)
            for k in range(KB):
                dve.wait_ge(proj_hi, k + 1)
                nc.vector.tensor_tensor(w_lo[:, k, :], wT_scaled[:, k, :], w_hi[:, k, :],
                                        ALU.subtract).then_inc(proj_lo, 1)
            for k in range(KB):
                low_part(0, k, z_hi_done, z_hi, z_lo, z_lo_done)
            dve.wait_ge(beta_applied, 1)
            nc.vector.tensor_tensor(bias_proj[:], slot[0][:, 0:NPROJ], par[:, PROJ_BIAS:PROJ_BIAS + NPROJ],
                                    ALU.add).then_inc(bias_summed, 1)
            dve.wait_ge(bias_summed, 1)
            nc.vector.tensor_scalar(bias_scaled[:], bias_proj[:], PROJ_SCALE, None, ALU.mult).then_inc(bias_ready, 1)
            dve.wait_ge(mean_abs, 1)
            nc.vector.tensor_scalar(threshold[:], slot[1][:, 0:2], TERNARY_EPS, 0.5,
                                    ALU.max, ALU.mult).then_inc(mean_floored, 1)
            dve.wait_ge(mean_floored, 1)
            nc.vector.tensor_scalar(minus_threshold[:], threshold[:], -1.0, None, ALU.mult).then_inc(threshold_ready, 1)
            dve.wait_ge(threshold_ready, 1)
            for m, (w, tern) in enumerate(((w1_rows, w1_tern), (w2_rows, w2_tern))):
                nc.vector.tensor_scalar(negatives[:, m, :], w, minus_threshold[:, m:m + 1], None,
                                        ALU.is_lt).then_inc(negatives_ready, 1)
                dve.wait_ge(negatives_ready, m + 1)
                nc.vector.scalar_tensor_tensor(tern, w, threshold[:, m:m + 1], negatives[:, m, :],
                                               ALU.is_gt, ALU.subtract).then_inc(ternary_ready, 1)
            for k in range(KB):
                low_part(0, k, x_hi_done, x_hi, x_lo, x_lo_done)
            for m, dst in enumerate((w1T, w2T)):
                dve.wait_ge(ternary_turned, m + 1)
                nc.vector.tensor_copy(dst[:].rearrange("p a b -> p (a b)"), slot[m][:].bitcast(F16)
                                      ).then_inc(ternary_placed, 1)
            dve.wait_ge(pool_consts, 4)

            def finish_rows(t, half):
                dve.wait_ge(out_turned, 2 * t + half + 1)
                n = SUBS // 2
                r = tile_rows(t, half * n, n)
                nc.vector.tensor_tensor(r, slot[half][:], r, ALU.add).then_inc(out_done, 1)

            def tile(t, first, last):
                if not first:
                    for half in range(2):
                        finish_rows(t - 1, half)
                if not last:
                    statistics(t + 1)
                n = KB * t
                for e in range(KB):
                    dve.wait_ge(gate_done, n + e + 1)
                    nc.vector.tensor_tensor_scan(decay[:, e, :], decay[:, e, :], zeros[:], 1.0,
                                                 ALU.mult, ALU.add).then_inc(decay_done, 1)
                for e in range(KB):
                    dve.wait_ge(decay_done, n + e + 1)
                    nc.vector.tensor_scalar(inverse[:, e, :], decay[:, e, :], SCAN_EPS, PROJ_SCALE * PROJ_SCALE,
                                            ALU.add, ALU.mult).then_inc(shifted_done, 1)
                for e in range(KB):
                    dve.wait_ge(shifted_done, n + e + 1)
                    nc.vector.reciprocal(inverse[:, e, :], inverse[:, e, :]).then_inc(inverse_done, 1)
                if not last:
                    dve.wait_ge(residual_done, 2 * t + 2)
                    first_norm(t + 1)
                for e in range(KB):
                    dve.wait_ge(inverse_done, n + e + 1)
                    dve.wait_ge(in_summed, n + e + 1)
                    nc.vector.scalar_tensor_tensor(state[:, e, :], slot[2 - 2 * e][:],
                                                   bias_scaled[:, KB + e:KB + e + 1], inverse[:, e, :],
                                                   ALU.add, ALU.mult).then_inc(term_done, 1)
                    dve.wait_ge(term_done, n + e + 1)
                    nc.vector.tensor_tensor_scan(state[:, e, :], state[:, e, :], zeros[:], 0.0,
                                                 ALU.add, ALU.add).then_inc(sum_done, 1)
                    dve.wait_ge(sum_done, n + e + 1)
                    nc.vector.scalar_tensor_tensor(state[:, e, :], state[:, e, :], state0_scaled[:, e:e + 1],
                                                   decay[:, e, :], ALU.add, ALU.mult).then_inc(state_done, 1)
                    dve.wait_ge(state_done, n + e + 1)
                    dve.wait_ge(read_summed, n + e + 1)
                    nc.vector.scalar_tensor_tensor(state[:, e, :], slot[3 - 2 * e][:],
                                                   bias_scaled[:, 2 * KB + e:2 * KB + e + 1], state[:, e, :],
                                                   ALU.add, ALU.mult).then_inc(read_done, 1)
                if not last:
                    for k in range(KB):
                        low_part(t + 1, k, z_hi_done, z_hi, z_lo, z_lo_done)

                def mix(e):
                    dve.wait_ge(read_done, n + e + 1)
                    dve.wait_ge(down_summed, n + e + 1)
                    nc.vector.scalar_tensor_tensor(state[:, e, :], slot[e][:], par[:, B2 + e:B2 + e + 1],
                                                   state[:, e, :], ALU.add, ALU.add).then_inc(mixed_done, 1)

                mix(0)
                if not last:
                    for k in range(KB):
                        low_part(t + 1, k, x_hi_done, x_hi, x_lo, x_lo_done)
                mix(1)

            tile(0, True, False)
            with dve.Fori(1, TILES - 1) as t:
                tile(t, False, False)
            tile(TILES - 1, False, True)
            for half in range(2):
                finish_rows(TILES - 1, half)


_INS = ["L0_attn_X", "L0_attn_Wa", "L0_attn_ba", "L0_attn_Wb", "L0_attn_bb", "L0_attn_Wc", "L0_attn_bc",
        "L0_attn_gamma", "L0_attn_beta", "L0_attn_h0", "L0_ffn_W1", "L0_ffn_b1", "L0_ffn_W2", "L0_ffn_b2"]


def kernel(**inputs):
    import numpy as _np
    import concourse.bacc as _bacc
    from concourse import mybir as _mybir
    from concourse.bass_utils import run_bass_kernel_spmd as _run

    nc = _bacc.Bacc("TRN2", target_bir_lowering=False, num_devices=1)
    arrays, args = {}, []
    for name in _INS:
        a = _np.ascontiguousarray(inputs[name])
        arrays[f"in_{name}_dram"] = a
        args.append(nc.dram_tensor(f"in_{name}_dram", a.shape, _mybir.dt.from_np(a.dtype), kind="ExternalInput").ap())
    shape = inputs["L0_attn_X"].shape
    args.append(nc.dram_tensor("out_dram", shape, _mybir.dt.float32, kind="ExternalOutput").ap())
    build(nc, *args)
    r = _run(nc, [arrays], core_ids=[0])
    return r.results[0]["out_dram"]
```

```python
from contextlib import ExitStack

import concourse.bass as bass
from concourse import mybir

P = 128
ALU = mybir.AluOpType
ACT = mybir.ActivationFunctionType
F32 = mybir.dt.float32
F16 = mybir.dt.float16

LN_EPS = 1e-5
SCAN_EPS = 1e-8
TERNARY_EPS = 1e-8

ROW_SCALE = 2.0**10
WEIGHT_SCALE = 2.0**6
PROJ_SCALE = ROW_SCALE * WEIGHT_SCALE
G_BUFFERS = 4
ZN_POOL = 4
PIECES = 4


def build(nc, X, Wa, ba, Wb, bb, Wc, bc, gamma, beta, h0, W1, b1, W2, b2, out):
    TILES, L, D = X.shape
    FF = W1.shape[0]
    SUBS = L // P
    KB = D // P
    FB = FF // P
    HALF = L // 2
    NPROJ = 3 * KB
    BN = 6
    assert L == 1024 and KB == 2 and FB == 8 and FF == L and TILES >= 3

    PROJ_BIAS, STATE0, B2, B1 = 0, NPROJ, NPROJ + KB, NPROJ + 2 * KB
    NPAR = B1 + FB

    x_rows = X.rearrange("b (s p) d -> p b s d", p=P)
    out_rows = out.rearrange("b (s p) d -> p b s d", p=P)

    with ExitStack() as ctx:

        def sb(name, shape, dt=F32):
            return ctx.enter_context(nc.sbuf_tensor(name, shape, dt))

        def sem(name):
            return ctx.enter_context(nc.semaphore(name))

        slot = [ctx.enter_context(nc.psum_tensor(f"slot{i}", [P, L], F32)) for i in range(4)]

        rows = sb("rows", [P, TILES * SUBS * D])
        xn = sb("xn", [P, SUBS, D])
        zn = sb("zn", [P, SUBS, D])
        x_hi = sb("x_hi", [P, SUBS, KB, P], F16)
        x_lo = sb("x_lo", [P, SUBS, KB, P], F16)
        z_hi = sb("z_hi", [P, SUBS, KB, P], F16)
        z_lo = sb("z_lo", [P, SUBS, KB, P], F16)
        decay = sb("decay", [P, KB, L])
        inverse = sb("inverse", [P, KB, L])
        state = sb("state", [P, KB, L])
        zeros = sb("zeros", [P, L])
        gelu = sb("gelu", [P, G_BUFFERS, L])
        g_hi = sb("g_hi", [P, FB, L], F16)
        g_lo = sb("g_lo", [P, FB, L], F16)
        bn = sb("bn", [P, SUBS, BN])
        halves = sb("halves", [P, 4, SUBS])
        mean_sum, mean_gap, square_sum, gap_square = (halves[:, i, :] for i in range(4))
        mean = sb("mean", [P, SUBS])
        var = sb("var", [P, SUBS])
        scalars = sb("scalars", [P, 6, SUBS])
        var_eps, both_eps, rstd, rstd_both, std, rstd_n = (scalars[:, i, :] for i in range(6))
        minus_half = sb("minus_half", [P, SUBS])
        row_scale = sb("row_scale", [P, SUBS])

        ident = sb("ident", [P, P])
        ident16 = sb("ident16", [P, P], F16)
        averager = sb("averager", [P, P])
        gamma_rows = sb("gamma_rows", [KB, P])
        beta_rows = sb("beta_rows", [P, D])
        beta_terms = sb("beta_terms", [P, 2, D])
        beta_sums = sb("beta_sums", [P, NPROJ])
        par_rows = sb("par_rows", [NPAR, P])
        par = sb("par", [P, NPAR])
        bias_proj = sb("bias_proj", [P, NPROJ])
        bias_scaled = sb("bias_scaled", [P, NPROJ])
        gamma_scaled = sb("gamma_scaled", [P, KB])
        state0_scaled = sb("state0_scaled", [P, KB])
        w_proj = sb("w_proj", [P, NPROJ, D])
        w_hi = sb("w_hi", [P, KB, NPROJ * P], F16)
        w_lo = sb("w_lo", [P, KB, NPROJ * P], F16)
        w1_rows = g_hi[:, 0:4, :].rearrange("p a b -> p (a b)").bitcast(F32)
        w1_tern = g_lo[:, 0:2, :].rearrange("p a b -> p (a b)")
        w1_below = g_lo[:, 2:4, :].rearrange("p a b -> p (a b)")
        w2_rows = state[:].rearrange("p a b -> p (a b)")
        w2_tern = sb("w2_tern", [P, FF * KB], F16)
        w2_held = sb("w2_held", [P, SUBS * D])
        z_hi_rows, z_lo_rows = (zn[:, i * SUBS // 2:(i + 1) * SUBS // 2, :].rearrange("p s d -> p (s d)").bitcast(F16)
                                for i in range(2))
        x_hi_rows, x_lo_rows = (w2_held[:, i * L:(i + 1) * L].bitcast(F16) for i in range(2))
        magnitudes = gelu[:, 0:2, :].rearrange("p a b -> p (a b)")
        abs_sums = sb("abs_sums", [P, 2])
        threshold = sb("threshold", [P, 2])
        minus_threshold = sb("minus_threshold", [P, 2])
        w1T = sb("w1T", [P, KB, FF], F16)
        w2T = sb("w2T", [P, FB, D], F16)

        piece_loaded = [sem(f"piece_loaded{i}") for i in range(PIECES)]
        x_loaded = sem("x_loaded")
        gamma_loaded = sem("gamma_loaded")
        beta_loaded = sem("beta_loaded")
        par_loaded = sem("par_loaded")
        proj_loaded = sem("proj_loaded")
        w1_loaded = sem("w1_loaded")
        w2_loaded = sem("w2_loaded")
        out_stored = sem("out_stored")
        pool_consts = sem("pool_consts")
        ident_started = sem("ident_started")
        ident_made = sem("ident_made")
        ident16_made = sem("ident16_made")
        par_turned = sem("par_turned")
        par_ready = sem("par_ready")
        par_scaled = sem("par_scaled")
        proj_turned = sem("proj_turned")
        proj_hi = sem("proj_hi")
        proj_lo = sem("proj_lo")
        beta_applied = sem("beta_applied")
        bias_summed = sem("bias_summed")
        bias_ready = sem("bias_ready")
        abs_summed = sem("abs_summed")
        mean_abs = sem("mean_abs")
        mean_floored = sem("mean_floored")
        threshold_ready = sem("threshold_ready")
        w1_compared = sem("w1_compared")
        ternary_ready = sem("ternary_ready")
        w2_held_done = sem("w2_held_done")
        w2_excess_done = sem("w2_excess_done")
        w2_ternary_ready = sem("w2_ternary_ready")
        w1_turned = sem("w1_turned")
        w1_placed = sem("w1_placed")
        w1_rest_placed = sem("w1_rest_placed")
        w2_turned = sem("w2_turned")
        w2_placed = sem("w2_placed")
        bn_done = sem("bn_done")
        halves_done = sem("halves_done")
        moments_done = sem("moments_done")
        scalars_done = sem("scalars_done")
        xn_done = sem("xn_done")
        zn_done = sem("zn_done")
        zn_pool_done = sem("zn_pool_done")
        residual_done = sem("residual_done")
        z_turned = sem("z_turned")
        x_turned = sem("x_turned")
        z_hi_done = sem("z_hi_done")
        z_lo_done = sem("z_lo_done")
        x_hi_done = sem("x_hi_done")
        x_lo_done = sem("x_lo_done")
        z_hi_made = sem("z_hi_made")
        z_lo_made = sem("z_lo_made")
        x_hi_made = sem("x_hi_made")
        x_lo_made = sem("x_lo_made")
        z_hi_turned = sem("z_hi_turned")
        z_lo_turned = sem("z_lo_turned")
        x_hi_turned = sem("x_hi_turned")
        x_lo_turned = sem("x_lo_turned")
        gate_summed = sem("gate_summed")
        gate_done = sem("gate_done")
        in_summed = sem("in_summed")
        read_summed = sem("read_summed")
        decay_done = sem("decay_done")
        shifted_done = sem("shifted_done")
        inverse_done = sem("inverse_done")
        term_done = sem("term_done")
        sum_done = sem("sum_done")
        state_done = sem("state_done")
        read_done = sem("read_done")
        up_summed = sem("up_summed")
        gelu_done = sem("gelu_done")
        g_hi_done = sem("g_hi_done")
        g_lo_done = sem("g_lo_done")
        down_summed = sem("down_summed")
        last_summed = sem("last_summed")
        mixed_done = sem("mixed_done")
        out_turned = sem("out_turned")
        out_done = sem("out_done")

        block = ctx.enter_context(nc.Block())

        def tile_rows(t, first, n):
            return rows[:, bass.ds(t * (SUBS * D) + first * D, n * D)]

        @block.sync
        def _(sp):
            n = SUBS // PIECES
            for i in range(PIECES):
                sp.dma_start(tile_rows(0, i * n, n).rearrange("p (s d) -> p s d", d=D),
                             x_rows[:, 0, i * n:(i + 1) * n, :]).then_inc(piece_loaded[i], 16)
            for i, w in enumerate((Wa, Wb, Wc)):
                sp.dma_start(w_proj[:, i * KB:(i + 1) * KB, :],
                             w.rearrange("(k p) d -> p k d", p=P)).then_inc(proj_loaded, 16)
            sp.dma_start(w1_rows.rearrange("p (f d) -> p f d", d=D),
                         W1.rearrange("(f p) d -> p f d", p=P)).then_inc(w1_loaded, 16)
            sp.dma_start(w2_rows.rearrange("p (k f) -> p k f", f=FF),
                         W2.rearrange("(k p) f -> p k f", p=P)).then_inc(w2_loaded, 16)
            for at, v in ((PROJ_BIAS, ba), (PROJ_BIAS + KB, bb), (PROJ_BIAS + 2 * KB, bc),
                          (STATE0, h0.rearrange("a d -> (a d)")), (B2, b2), (B1, b1)):
                n = v.shape[0] // P
                sp.dma_start(par_rows[at:at + n, :], v.rearrange("(k p) -> k p", p=P)).then_inc(par_loaded, 16)
            sp.wait_ge(w2_loaded, 16)
            for t in range(1, TILES):
                if t > 1:
                    sp.wait_ge(x_loaded, 16 * (t - 1))
                sp.dma_start(tile_rows(t, 0, SUBS).rearrange("p (s d) -> p s d", d=D),
                             x_rows[:, t]).then_inc(x_loaded, 16)

            def store(t):
                for half in range(2):
                    sp.wait_ge(out_done, t * 2 + half + 1)
                    n = SUBS // 2
                    sp.dma_start(out_rows[:, t, half * n:(half + 1) * n, :],
                                 tile_rows(t, half * n, n).rearrange("p (s d) -> p s d", d=D)
                                 ).then_inc(out_stored, 16)

            def turn_parts(t):
                sp.wait_ge(read_summed, KB * t + KB)
                for src, dst, made, count, turned in (
                        (z_hi_rows, z_hi, z_hi_made, SUBS * t + SUBS, z_hi_turned),
                        (x_hi_rows, x_hi, x_hi_made, t + 1, x_hi_turned),
                        (z_lo_rows, z_lo, z_lo_made, SUBS * t + SUBS, z_lo_turned),
                        (x_lo_rows, x_lo, x_lo_made, t + 1, x_lo_turned)):
                    sp.wait_ge(made, count)
                    sp.dma_start_transpose(dst[:].rearrange("p s k q -> p (s k) q"), src).then_inc(turned, 16)

            for t in range(TILES):
                if t >= 1:
                    store(t - 1)
                if t < TILES - 1:
                    turn_parts(t)
            store(TILES - 1)
            sp.wait_ge(out_stored, 16 * 2 * TILES)

        @block.gpsimd
        def _(pool):
            nc.gpsimd.memset(ident[:], 0.0).then_inc(ident_started, 1)
            pool.wait_ge(ident_started, 1)
            nc.gpsimd.affine_select(out=ident[:], in_=ident[:], compare_op=ALU.not_equal, fill=1.0,
                                    base=0, pattern=[[-1, P]], channel_multiplier=1).then_inc(ident_made, 1)
            nc.gpsimd.memset(minus_half[:], -0.5).then_inc(pool_consts, 1)
            nc.gpsimd.memset(row_scale[:], ROW_SCALE).then_inc(pool_consts, 1)
            nc.gpsimd.memset(averager[:], 1.0 / (FF * D)).then_inc(pool_consts, 1)
            nc.gpsimd.memset(zeros[:], 0.0).then_inc(pool_consts, 1)

            def norm_scalars(g, s0=0, s1=SUBS):
                n = 5 * g
                c = slice(s0, s1)
                pool.wait_ge(moments_done, 4 * g + 4)
                nc.gpsimd.tensor_tensor(rstd[:, c], var_eps[:, c], minus_half[:, c], ALU.pow).then_inc(scalars_done, 1)
                nc.gpsimd.tensor_tensor(rstd_both[:, c], both_eps[:, c], minus_half[:, c],
                                        ALU.pow).then_inc(scalars_done, 1)
                pool.wait_ge(scalars_done, n + 2)
                nc.gpsimd.tensor_tensor(std[:, c], var_eps[:, c], rstd[:, c], ALU.mult).then_inc(scalars_done, 1)
                nc.gpsimd.tensor_tensor(rstd_both[:, c], rstd_both[:, c], row_scale[:, c],
                                        ALU.mult).then_inc(scalars_done, 1)
                pool.wait_ge(scalars_done, n + 4)
                nc.gpsimd.tensor_tensor(rstd_n[:, c], rstd_both[:, c], std[:, c], ALU.mult).then_inc(scalars_done, 1)

            def residuals(t):
                for half in range(2):
                    n = SUBS // 2
                    pool.wait_ge(xn_done, SUBS * t + n * (half + 1))
                    r = tile_rows(t, half * n, n)
                    nc.gpsimd.tensor_tensor(r, r, xn[:, half * n:(half + 1) * n, :].rearrange("p s d -> p (s d)"),
                                            ALU.add).then_inc(residual_done, 1)

            def tile(t, last):
                for f in range(FB):
                    if f == G_BUFFERS and not last:
                        norm_scalars(t + 2)
                    pool.wait_ge(g_hi_done, FB * t + f + 1)
                    nc.gpsimd.tensor_tensor(g_lo[:, f, :], gelu[:, f % G_BUFFERS, :], g_hi[:, f, :],
                                            ALU.subtract).then_inc(g_lo_done, 1)
                if not last:
                    residuals(t + 1)

            pool.wait_ge(pool_consts, 2)
            norm_scalars(0, 0, SUBS // 2)
            norm_scalars(1, SUBS // 2, SUBS)
            pool.wait_ge(scalars_done, 10)
            for s in range(SUBS - ZN_POOL, SUBS):
                pool.wait_ge(xn_done, s + 1)
                nc.gpsimd.tensor_scalar(zn[:, s, :], xn[:, s, :], rstd_n[:, s:s + 1], 1.0,
                                        ALU.mult, ALU.mult).then_inc(zn_pool_done, 1)
            residuals(0)
            pool.wait_ge(threshold_ready, 2)
            nc.gpsimd.tensor_scalar(w2_held[:], w2_rows, threshold[:, 1:2], minus_threshold[:, 1:2],
                                    ALU.min, ALU.max).then_inc(w2_held_done, 1)
            pool.wait_ge(w2_held_done, 1)
            nc.gpsimd.tensor_tensor(w2_held[:], w2_rows, w2_held[:], ALU.subtract).then_inc(w2_excess_done, 1)
            tile(0, False)
            with pool.Fori(1, TILES - 1) as t:
                tile(t, False)
            tile(TILES - 1, True)

        @block.scalar
        def _(act):
            act.dma_start(gamma_rows[:], gamma.rearrange("(k p) -> k p", p=P)).then_inc(gamma_loaded, 16)
            act.dma_start(beta_rows[:], beta.rearrange("(a d) -> a d", a=1).broadcast_to([P, D])
                          ).then_inc(beta_loaded, 16)
            act.wait_ge(ident_made, 1)
            nc.scalar.copy(ident16[:], ident[:]).then_inc(ident16_made, 1)

            def high_part(k, turned, hi, done, at, scale):
                act.wait_ge(turned, k + 1)
                nc.scalar.activation(hi[:, :, k, :], slot[at + k][:].rearrange("p (s q) -> p s q", q=P), ACT.Copy,
                                     scale=scale).then_inc(done, 1)

            act.wait_ge(scalars_done, 5)
            for s in range(SUBS - ZN_POOL):
                act.wait_ge(xn_done, s + 1)
                nc.scalar.mul(zn[:, s, :], xn[:, s, :], rstd_n[:, s:s + 1]).then_inc(zn_done, 1)
            act.wait_ge(par_scaled, 1)
            for k in range(KB):
                act.wait_ge(proj_turned, k + 1)
                nc.scalar.activation(w_hi[:, k, :], slot[k][:, 0:NPROJ * P], ACT.Copy,
                                     scale=gamma_scaled[:, k:k + 1]).then_inc(proj_hi, 1)

            def magnitude_sums(m, w, loaded):
                act.wait_ge(loaded, 16)
                if m:
                    act.wait_ge(abs_summed, m)
                nc.scalar.activation(magnitudes, w, ACT.Abs, accum_out=abs_sums[:, m:m + 1]).then_inc(abs_summed, 1)

            magnitude_sums(0, w1_rows, w1_loaded)
            for k in range(KB):
                high_part(k, x_turned, x_hi, x_hi_done, 2, ROW_SCALE)
            for k in range(KB):
                high_part(k, z_turned, z_hi, z_hi_done, 0, 1.0)
            magnitude_sums(1, w2_rows, w2_loaded)

            def tile(t, first, last):
                for e in range(KB):
                    if first and e == 1:
                        act.wait_ge(w1_turned, 1)
                        nc.scalar.copy(w1T[:, 0, :], slot[0][:, 0:HALF].bitcast(F16)).then_inc(w1_placed, 1)
                    act.wait_ge(gate_summed, KB * t + e + 1)
                    nc.scalar.activation(decay[:, e, :], slot[2 + e][:], ACT.Sigmoid, bias=bias_proj[:, e:e + 1],
                                         scale=1.0 / PROJ_SCALE).then_inc(gate_done, 1)

                def g_high(f):
                    act.wait_ge(gelu_done, FB * t + f + 1)
                    nc.scalar.copy(g_hi[:, f, :], gelu[:, f % G_BUFFERS, :]).then_inc(g_hi_done, 1)

                for f in range(FB):
                    act.wait_ge(up_summed, FB * t + f + 1)
                    if f >= G_BUFFERS:
                        act.wait_ge(g_lo_done, FB * t + f - G_BUFFERS + 1)
                    nc.scalar.activation(gelu[:, f % G_BUFFERS, :], slot[f % 4][:], ACT.Gelu,
                                         bias=par[:, B1 + f:B1 + f + 1], scale=1.0 / ROW_SCALE).then_inc(gelu_done, 1)
                    if f >= 1:
                        g_high(f - 1)
                g_high(FB - 1)
                if first:
                    act.wait_ge(w2_excess_done, 1)
                    nc.scalar.activation(w2_tern[:], w2_held[:], ACT.Sign).then_inc(w2_ternary_ready, 1)
                    act.wait_ge(w2_turned, 1)
                    nc.scalar.copy(w2T[:].rearrange("p a b -> p (a b)"), slot[1][:].bitcast(F16)
                                   ).then_inc(w2_placed, 1)
                if not last:
                    act.wait_ge(scalars_done, 5 * t + 15)
                    for s in range(SUBS):
                        act.wait_ge(xn_done, SUBS * t + SUBS + s + 1)
                        nc.scalar.mul(z_hi_rows[:, s * D:(s + 1) * D], xn[:, s, :], rstd_n[:, s:s + 1]
                                      ).then_inc(z_hi_made, 1)
                    nc.scalar.activation(x_hi_rows, xn[:].rearrange("p s d -> p (s d)"), ACT.Copy,
                                         scale=ROW_SCALE).then_inc(x_hi_made, 1)

            act.wait_ge(bias_ready, 1)
            tile(0, True, False)
            with act.Fori(1, TILES - 1) as t:
                tile(t, False, False)
            tile(TILES - 1, False, True)

        @block.tensor
        def _(pe):
            def turn_norm(k, src, turned, at):
                for s in range(SUBS):
                    mm = nc.tensor.transpose(slot[at + k][:, s * P:(s + 1) * P], src[:, s, k * P:(k + 1) * P], ident[:])
                mm.then_inc(turned, 1)

            def half_subs(half):
                return slice(half * SUBS // 2, (half + 1) * SUBS // 2)

            def project(dst, j, summed, low=None):
                passes = [(w, z, k) for w, z in ((w_hi, z_hi), (w_lo, z_hi), (w_hi, z_lo)) for k in range(KB)]
                for n, (w, z, k) in enumerate(passes):
                    if low is not None and n == 2 * KB:
                        pe.wait_ge(*low)
                    for half in range(2):
                        c = slice(half * HALF, (half + 1) * HALF)
                        mm = nc.tensor.matmul(dst[:, c], w[:, k, j * P:(j + 1) * P], z[:, half_subs(half), k, :],
                                              start=(n == 0), stop=(n == len(passes) - 1))
                mm.then_inc(summed, 1)

            pe.wait_ge(ident_made, 1)
            pe.wait_ge(gamma_loaded, 16)
            nc.tensor.transpose(slot[2][:, 0:KB], gamma_rows[:], ident[0:KB, 0:KB]).then_inc(par_turned, 1)
            pe.wait_ge(proj_loaded, 16 * 3)
            for k in range(KB):
                for j in range(NPROJ):
                    mm = nc.tensor.transpose(slot[k][:, j * P:(j + 1) * P], w_proj[:, j, k * P:(k + 1) * P], ident[:])
                mm.then_inc(proj_turned, 1)

            def average_magnitude(m, at):
                pe.wait_ge(abs_summed, m + 1)
                nc.tensor.matmul(slot[at][:, 0:1], averager[:], abs_sums[:, m:m + 1],
                                 start=True, stop=True).then_inc(mean_abs, 1)

            def turn_w1():
                pe.wait_ge(ident16_made, 1)
                pe.wait_ge(ternary_ready, 1)
                turned = slot[0][:].bitcast(F16)
                for k in range(KB):
                    for f in range(FB):
                        mm = nc.tensor.transpose(turned[:, k * FF + f * P:k * FF + (f + 1) * P],
                                                 w1_tern[:, f * D + k * P:f * D + (k + 1) * P], ident16[:])
                mm.then_inc(w1_turned, 1)

            def turn_w2():
                pe.wait_ge(w2_ternary_ready, 1)
                turned = slot[1][:].bitcast(F16)
                for f in range(FB):
                    for k in range(KB):
                        mm = nc.tensor.transpose(turned[:, f * D + k * P:f * D + (k + 1) * P],
                                                 w2_tern[:, k * FF + f * P:k * FF + (f + 1) * P], ident16[:])
                mm.then_inc(w2_turned, 1)

            pe.wait_ge(par_scaled, 1)
            pe.wait_ge(xn_done, SUBS)
            turn_norm(0, xn, x_turned, 2)
            turn_norm(1, xn, x_turned, 2)
            pe.wait_ge(proj_lo, 1)
            pe.wait_ge(zn_pool_done, ZN_POOL)
            pe.wait_ge(zn_done, SUBS - ZN_POOL)
            turn_norm(0, zn, z_turned, 0)
            pe.wait_ge(pool_consts, 3)
            pe.wait_ge(proj_lo, 2)
            average_magnitude(0, 1)
            pe.wait_ge(mean_floored, 1)
            turn_norm(1, zn, z_turned, 0)

            def turn_small():
                pe.wait_ge(z_lo_done, KB)
                pe.wait_ge(par_loaded, 16 * 6)
                nc.tensor.transpose(slot[1][:, HALF:HALF + NPAR], par_rows[:], ident[0:NPAR, 0:NPAR]
                                    ).then_inc(par_turned, 1)
                average_magnitude(1, 1)

            def turn_out(t, half, mixed, at=0):
                pe.wait_ge(mixed_done, mixed)
                for s in range(SUBS // 2):
                    for e in range(KB):
                        tok = (half * (SUBS // 2) + s) * P
                        mm = nc.tensor.transpose(slot[at + half][:, s * D + e * P:s * D + (e + 1) * P],
                                                 state[:, e, tok:tok + P], ident[:])
                mm.then_inc(out_turned, 1)

            def down(t, k, dst, halves, summed):
                for f in range(FB):
                    pe.wait_ge(g_lo_done, FB * t + f + 1)
                    for g in (g_hi, g_lo):
                        for half in halves:
                            c = slice(half * HALF, (half + 1) * HALF)
                            mm = nc.tensor.matmul(dst[:, c], w2T[:, f, k * P:(k + 1) * P], g[:, f, c],
                                                  start=(f == 0 and g is g_hi), stop=(f == FB - 1 and g is g_lo))
                mm.then_inc(summed, 1)

            def tile(t, first, last):
                for e in range(KB):
                    if first:
                        pe.wait_ge(z_hi_done, KB)
                        pe.wait_ge(x_lo_done, e + 1)
                        project(slot[2 + e], e, gate_summed, low=(z_lo_done, KB))
                    else:
                        pe.wait_ge(z_hi_turned, 16 * t)
                        pe.wait_ge(mixed_done, KB * t - KB + e + 1)
                        project(slot[2 + e], e, gate_summed, low=(z_lo_turned, 16 * t))
                    if first and e == 0:
                        turn_small()
                if first:
                    turn_w1()
                for f in range(FB):
                    if f < 2:
                        if first:
                            pe.wait_ge(w1_placed, 1)
                            pe.wait_ge(w1_rest_placed, 1)
                            pe.wait_ge(par_ready, 1)
                            pe.wait_ge(mean_floored, 2)
                        else:
                            pe.wait_ge(x_hi_turned, 16 * t)
                            pe.wait_ge(x_lo_turned, 16 * t)
                            pe.wait_ge((term_done, read_done)[f], KB * t)
                    elif f < 4:
                        pe.wait_ge(gate_done, KB * t + f - 2 + 1)
                    else:
                        pe.wait_ge(gelu_done, FB * t + f - 4 + 1)
                    dst = slot[f % 4]
                    for k in range(KB):
                        for n, xs in enumerate((x_hi, x_lo)):
                            for half in range(2):
                                c = slice(half * HALF, (half + 1) * HALF)
                                mm = nc.tensor.matmul(dst[:, c], w1T[:, k, f * P:(f + 1) * P], xs[:, half_subs(half), k, :],
                                                      start=(k == 0 and n == 0), stop=(k == KB - 1 and n == 1))
                    mm.then_inc(up_summed, 1)
                if not first:
                    for half in range(2):
                        pe.wait_ge(gelu_done, FB * t + 5 + half)
                        turn_out(t - 1, half, KB * t)
                pe.wait_ge(gelu_done, FB * t + 7)
                project(slot[2], KB, in_summed)
                pe.wait_ge(gelu_done, FB * t + 8)
                project(slot[3], 2 * KB, read_summed)
                if first:
                    turn_w2()
                else:
                    pe.wait_ge(out_done, 2 * t - 1)
                project(slot[0], KB + 1, in_summed)
                if first:
                    pe.wait_ge(w2_placed, 1)
                else:
                    pe.wait_ge(out_done, 2 * t)
                project(slot[1], 2 * KB + 1, read_summed)
                if not last:
                    pe.wait_ge(term_done, KB * t + 1)
                    down(t, 0, slot[2], (0, 1), down_summed)
                    pe.wait_ge(read_done, KB * t + 1)
                    down(t, 1, slot[3], (0, 1), down_summed)

            tile(0, True, False)
            with pe.Fori(1, TILES - 1) as t:
                tile(t, False, False)
            t = TILES - 1
            tile(t, False, True)
            for half in range(2):
                for k in range(KB):
                    if half == 0:
                        pe.wait_ge((term_done, read_done)[k], KB * t + 2)
                    down(t, k, slot[k], (half,), last_summed)
                    if half == 1 and k == 0:
                        turn_out(t, 0, KB * t + 2, at=2)
            turn_out(t, 1, KB * t + 4, at=2)

        @block.vector
        def _(dve):
            def statistics(t):
                dve.wait_ge(x_loaded, 16 * t)
                for s in range(SUBS):
                    nc.vector.bn_stats(bn[:, s, :], tile_rows(t, s, 1)).then_inc(bn_done, 1)

            ALL = slice(0, SUBS)

            def sums(g, c=ALL):
                dve.wait_ge(bn_done, SUBS * g if c == ALL else c.stop)
                nc.vector.tensor_tensor(mean_gap[:, c], bn[:, c, 1], bn[:, c, 4], ALU.subtract).then_inc(halves_done, 1)
                nc.vector.tensor_tensor(mean_sum[:, c], bn[:, c, 1], bn[:, c, 4], ALU.add).then_inc(halves_done, 1)
                nc.vector.tensor_tensor(square_sum[:, c], bn[:, c, 2], bn[:, c, 5], ALU.add).then_inc(halves_done, 1)

            def means(g, c=ALL):
                dve.wait_ge(halves_done, 4 * g + 1)
                nc.vector.scalar_tensor_tensor(gap_square[:, c], mean_gap[:, c], 0.25, mean_gap[:, c],
                                               ALU.mult, ALU.mult).then_inc(halves_done, 1)
                dve.wait_ge(halves_done, 4 * g + 2)
                nc.vector.tensor_scalar(mean[:, c], mean_sum[:, c], 0.5, None, ALU.mult).then_inc(moments_done, 1)

            def variances(g, c=ALL):
                dve.wait_ge(halves_done, 4 * g + 4)
                nc.vector.scalar_tensor_tensor(var[:, c], square_sum[:, c], 1.0 / D, gap_square[:, c],
                                               ALU.mult, ALU.add).then_inc(moments_done, 1)

            def variances_eps(g, c=ALL):
                dve.wait_ge(moments_done, 4 * g + 2)
                nc.vector.tensor_scalar(var_eps[:, c], var[:, c], LN_EPS, None, ALU.add).then_inc(moments_done, 1)

            def variances_both_eps(g, c=ALL):
                dve.wait_ge(moments_done, 4 * g + 3)
                nc.vector.scalar_tensor_tensor(both_eps[:, c], var_eps[:, c], LN_EPS, var[:, c],
                                               ALU.mult, ALU.add).then_inc(moments_done, 1)

            def first_norm(g, t, s0=0, s1=SUBS):
                dve.wait_ge(scalars_done, 5 * g + 1)
                for s in range(s0, s1):
                    nc.vector.tensor_scalar(xn[:, s, :], tile_rows(t, s, 1), mean[:, s:s + 1], rstd[:, s:s + 1],
                                            ALU.subtract, ALU.mult).then_inc(xn_done, 1)

            def low_part(k, hi_done, hi, lo, done, at, scale):
                dve.wait_ge(hi_done, k + 1)
                nc.vector.scalar_tensor_tensor(lo[:, :, k, :], slot[at + k][:].rearrange("p (s q) -> p s q", q=P),
                                               scale, hi[:, :, k, :], ALU.mult, ALU.subtract).then_inc(done, 1)

            for g in range(2):
                for s in range(g * SUBS // 2, (g + 1) * SUBS // 2):
                    if s % (SUBS // PIECES) == 0:
                        dve.wait_ge(piece_loaded[s // (SUBS // PIECES)], 16)
                    nc.vector.bn_stats(bn[:, s, :], tile_rows(0, s, 1)).then_inc(bn_done, 1)
                for step in (sums, means, variances, variances_eps, variances_both_eps):
                    step(g, slice(g * SUBS // 2, (g + 1) * SUBS // 2))
            dve.wait_ge(par_turned, 1)
            nc.vector.tensor_scalar(gamma_scaled[:], slot[2][:, 0:KB], WEIGHT_SCALE, None,
                                    ALU.mult).then_inc(par_scaled, 1)
            first_norm(0, 0, 0, SUBS // 2)
            first_norm(1, 0, SUBS // 2, SUBS)
            for k in range(KB):
                dve.wait_ge(proj_hi, k + 1)
                nc.vector.scalar_tensor_tensor(w_lo[:, k, :], slot[k][:, 0:NPROJ * P], gamma_scaled[:, k:k + 1],
                                               w_hi[:, k, :], ALU.mult, ALU.subtract).then_inc(proj_lo, 1)
            dve.wait_ge(beta_loaded, 16)
            dve.wait_ge(proj_loaded, 16 * 3)
            for j in range(NPROJ):
                if j >= 2:
                    dve.wait_ge(beta_applied, j - 1)
                nc.vector.scalar_tensor_tensor(beta_terms[:, j % 2, :], w_proj[:, j, :], 1.0, beta_rows[:],
                                               ALU.mult, ALU.mult, accum_out=beta_sums[:, j:j + 1]
                                               ).then_inc(beta_applied, 1)
            def thresholds(m, at):
                dve.wait_ge(mean_abs, m + 1)
                nc.vector.tensor_scalar(threshold[:, m:m + 1], slot[at][:, 0:1], TERNARY_EPS, 0.5,
                                        ALU.max, ALU.mult).then_inc(mean_floored, 1)
                dve.wait_ge(mean_floored, m + 1)
                nc.vector.tensor_scalar(minus_threshold[:, m:m + 1], threshold[:, m:m + 1], -1.0, None,
                                        ALU.mult).then_inc(threshold_ready, 1)

            thresholds(0, 1)
            for k in range(KB):
                low_part(k, x_hi_done, x_hi, x_lo, x_lo_done, 2, ROW_SCALE)
            for k in range(KB):
                low_part(k, z_hi_done, z_hi, z_lo, z_lo_done, 0, 1.0)
            dve.wait_ge(threshold_ready, 1)
            nc.vector.tensor_scalar(w1_below, w1_rows, minus_threshold[:, 0:1], None,
                                    ALU.is_lt).then_inc(w1_compared, 1)
            dve.wait_ge(par_turned, 2)
            nc.vector.tensor_copy(par[:], slot[1][:, HALF:HALF + NPAR]).then_inc(par_ready, 1)
            thresholds(1, 1)
            dve.wait_ge(beta_applied, NPROJ)
            dve.wait_ge(par_ready, 1)
            nc.vector.tensor_tensor(bias_proj[:], beta_sums[:], par[:, PROJ_BIAS:PROJ_BIAS + NPROJ],
                                    ALU.add).then_inc(bias_summed, 1)
            nc.vector.tensor_scalar(state0_scaled[:], par[:, STATE0:STATE0 + KB], 1.0 / PROJ_SCALE, None,
                                    ALU.mult).then_inc(par_scaled, 1)
            dve.wait_ge(bias_summed, 1)
            nc.vector.tensor_scalar(bias_scaled[:], bias_proj[:], PROJ_SCALE, None, ALU.mult).then_inc(bias_ready, 1)
            dve.wait_ge(w1_compared, 1)
            nc.vector.scalar_tensor_tensor(w1_tern, w1_rows, threshold[:, 0:1], w1_below,
                                           ALU.is_gt, ALU.subtract).then_inc(ternary_ready, 1)
            dve.wait_ge(pool_consts, 4)

            def decay_product(t, e):
                dve.wait_ge(gate_done, KB * t + e + 1)
                nc.vector.tensor_tensor_scan(decay[:, e, :], decay[:, e, :], zeros[:], 1.0,
                                             ALU.mult, ALU.add).then_inc(decay_done, 1)

            def shift_decay(t, e):
                dve.wait_ge(decay_done, KB * t + e + 1)
                nc.vector.tensor_scalar(inverse[:, e, :], decay[:, e, :], SCAN_EPS, PROJ_SCALE * PROJ_SCALE,
                                        ALU.add, ALU.mult).then_inc(shifted_done, 1)

            def invert_decay(t, e):
                dve.wait_ge(shifted_done, KB * t + e + 1)
                nc.vector.reciprocal(inverse[:, e, :], inverse[:, e, :]).then_inc(inverse_done, 1)

            decay_product(0, 0)
            dve.wait_ge(w1_turned, 1)
            nc.vector.tensor_copy(w1T[:, 1, :], slot[0][:, HALF:L].bitcast(F16)).then_inc(w1_rest_placed, 1)

            def finish_rows(t, half, at=0):
                dve.wait_ge(out_turned, 2 * t + half + 1)
                n = SUBS // 2
                r = tile_rows(t, half * n, n)
                nc.vector.tensor_tensor(r, slot[at + half][:], r, ALU.add).then_inc(out_done, 1)

            def tile(t, first, last):
                if not last and not first:
                    statistics(t + 1)
                n = KB * t
                in_slot, read_slot = (2, 0), (3, 1)
                if not first:
                    decay_product(t, 0)
                    if not last:
                        sums(t + 2)
                shift_decay(t, 0)
                if not last and not first:
                    means(t + 2)
                invert_decay(t, 0)
                if first:
                    statistics(1)
                    sums(2)
                    means(2)
                if not last:
                    variances(t + 2)
                decay_product(t, 1)
                if not last:
                    variances_eps(t + 2)
                shift_decay(t, 1)
                if not last:
                    variances_both_eps(t + 2)
                invert_decay(t, 1)
                if not last:
                    dve.wait_ge(residual_done, 2 * t + 2)
                    first_norm(t + 2, t + 1)
                if not first:
                    for half in range(2):
                        finish_rows(t - 1, half)
                for e in range(KB):
                    dve.wait_ge(inverse_done, n + e + 1)
                    dve.wait_ge(in_summed, n + e + 1)
                    nc.vector.scalar_tensor_tensor(state[:, e, :], slot[in_slot[e]][:],
                                                   bias_scaled[:, KB + e:KB + e + 1], inverse[:, e, :],
                                                   ALU.add, ALU.mult).then_inc(term_done, 1)
                    dve.wait_ge(term_done, n + e + 1)
                    nc.vector.tensor_tensor_scan(state[:, e, :], state[:, e, :], zeros[:], 0.0,
                                                 ALU.add, ALU.add).then_inc(sum_done, 1)
                    dve.wait_ge(sum_done, n + e + 1)
                    nc.vector.scalar_tensor_tensor(state[:, e, :], state[:, e, :], state0_scaled[:, e:e + 1],
                                                   decay[:, e, :], ALU.add, ALU.mult).then_inc(state_done, 1)
                    dve.wait_ge(state_done, n + e + 1)
                    dve.wait_ge(read_summed, n + e + 1)
                    nc.vector.scalar_tensor_tensor(state[:, e, :], slot[read_slot[e]][:],
                                                   bias_scaled[:, 2 * KB + e:2 * KB + e + 1], state[:, e, :],
                                                   ALU.add, ALU.mult).then_inc(read_done, 1)
                if not last:
                    for s in range(SUBS):
                        dve.wait_ge(z_hi_made, SUBS * t + s + 1)
                        nc.vector.scalar_tensor_tensor(z_lo_rows[:, s * D:(s + 1) * D], xn[:, s, :], rstd_n[:, s:s + 1],
                                                       z_hi_rows[:, s * D:(s + 1) * D], ALU.mult, ALU.subtract
                                                       ).then_inc(z_lo_made, 1)
                    dve.wait_ge(x_hi_made, t + 1)
                    nc.vector.scalar_tensor_tensor(x_lo_rows, xn[:].rearrange("p s d -> p (s d)"), ROW_SCALE,
                                                   x_hi_rows, ALU.mult, ALU.subtract).then_inc(x_lo_made, 1)
                    dve.wait_ge(read_done, n + KB)
                    for e in range(KB):
                        mix(e, slot[2 + e], slice(0, L), down_summed, n + e + 1)

            def mix(e, src, c, summed, count):
                dve.wait_ge(summed, count)
                nc.vector.scalar_tensor_tensor(state[:, e, c], src[:, c], par[:, B2 + e:B2 + e + 1],
                                               state[:, e, c], ALU.add, ALU.add).then_inc(mixed_done, 1)

            tile(0, True, False)
            with dve.Fori(1, TILES - 1) as t:
                tile(t, False, False)
            t = TILES - 1
            tile(t, False, True)
            dve.wait_ge(read_done, KB * t + KB)
            for half in range(2):
                for e in range(KB):
                    mix(e, slot[e], slice(half * HALF, (half + 1) * HALF), last_summed, KB * half + e + 1)
                    if half == 1 and e == 0:
                        finish_rows(t, 0, at=2)
            finish_rows(t, 1, at=2)


_INS = ["L0_attn_X", "L0_attn_Wa", "L0_attn_ba", "L0_attn_Wb", "L0_attn_bb", "L0_attn_Wc", "L0_attn_bc",
        "L0_attn_gamma", "L0_attn_beta", "L0_attn_h0", "L0_ffn_W1", "L0_ffn_b1", "L0_ffn_W2", "L0_ffn_b2"]


def kernel(**inputs):
    import numpy as _np
    import concourse.bacc as _bacc
    from concourse import mybir as _mybir
    from concourse.bass_utils import run_bass_kernel_spmd as _run

    nc = _bacc.Bacc("TRN2", target_bir_lowering=False, num_devices=1)
    arrays, args = {}, []
    for name in _INS:
        a = _np.ascontiguousarray(inputs[name])
        arrays[f"in_{name}_dram"] = a
        args.append(nc.dram_tensor(f"in_{name}_dram", a.shape, _mybir.dt.from_np(a.dtype), kind="ExternalInput").ap())
    shape = inputs["L0_attn_X"].shape
    args.append(nc.dram_tensor("out_dram", shape, _mybir.dt.float32, kind="ExternalOutput").ap())
    build(nc, *args)
    r = _run(nc, [arrays], core_ids=[0])
    return r.results[0]["out_dram"]
```

```python
from contextlib import ExitStack

import concourse.bass as bass
from concourse import mybir

P = 128
ALU = mybir.AluOpType
ACT = mybir.ActivationFunctionType
F32 = mybir.dt.float32
F16 = mybir.dt.float16
U16 = mybir.dt.uint16

LN_EPS = 1e-5
SCAN_EPS = 1e-8
TERNARY_EPS = 1e-8

ROW_SCALE = 2.0**10
WEIGHT_SCALE = 2.0**6
PROJ_SCALE = ROW_SCALE * WEIGHT_SCALE
G_BUFFERS = 4
LAST_PIECES = ((0, 4), (4, 2), (6, 2))
ZN_POOL = 4
PIECES = 4


def build(nc, X, Wa, ba, Wb, bb, Wc, bc, gamma, beta, h0, W1, b1, W2, b2, out):
    TILES, L, D = X.shape
    FF = W1.shape[0]
    SUBS = L // P
    KB = D // P
    FB = FF // P
    HALF = L // 2
    NPROJ = 3 * KB
    BN = 6
    assert L == 1024 and KB == 2 and FB == 8 and D == 2 * P and FF == L and TILES >= 3

    PROJ_BIAS, STATE0, B2, B1 = 0, NPROJ, NPROJ + KB, NPROJ + 2 * KB
    NPAR = B1 + FB

    x_rows = X.rearrange("b (s p) d -> p b s d", p=P)
    out_rows = out.rearrange("b (s p) d -> p b s d", p=P)

    with ExitStack() as ctx:

        def sb(name, shape, dt=F32):
            return ctx.enter_context(nc.sbuf_tensor(name, shape, dt))

        def sem(name):
            return ctx.enter_context(nc.semaphore(name))

        slot = [ctx.enter_context(nc.psum_tensor(f"slot{i}", [P, L], F32)) for i in range(4)]

        rows = sb("rows", [P, TILES * SUBS * D])
        xn = sb("xn", [P, SUBS, D])
        zn = sb("zn", [P, SUBS, D])
        x_hi = sb("x_hi", [P, SUBS, KB, P], F16)
        x_lo = sb("x_lo", [P, SUBS, KB, P], F16)
        z_hi = sb("z_hi", [P, SUBS, KB, P], F16)
        z_lo = sb("z_lo", [P, SUBS, KB, P], F16)
        decay = sb("decay", [P, KB, L])
        inverse = sb("inverse", [P, KB, L])
        state = sb("state", [P, KB, L])
        zeros = sb("zeros", [P, L])
        gelu = sb("gelu", [P, G_BUFFERS, L])
        g_hi = sb("g_hi", [P, FB, L], F16)
        g_lo = sb("g_lo", [P, FB, L], F16)
        bn = sb("bn", [P, SUBS, BN])
        halves = sb("halves", [P, 4, SUBS])
        mean_sum, mean_gap, square_sum, gap_square = (halves[:, i, :] for i in range(4))
        mean = sb("mean", [P, SUBS])
        var = sb("var", [P, SUBS])
        scalars = sb("scalars", [P, 6, SUBS])
        var_eps, both_eps, rstd, rstd_both, std, rstd_n = (scalars[:, i, :] for i in range(6))
        minus_half = sb("minus_half", [P, SUBS])
        row_scale = sb("row_scale", [P, SUBS])

        ident = sb("ident", [P, P])
        ident16 = sb("ident16", [P, P], F16)
        averager = sb("averager", [P, P])
        gamma_rows = sb("gamma_rows", [KB, P])
        beta_rows = sb("beta_rows", [P, D])
        beta_copy = sb("beta_copy", [P, 2, D])
        beta_sums = sb("beta_sums", [P, NPROJ])
        par_rows = sb("par_rows", [NPAR, P])
        par = sb("par", [P, NPAR])
        bias_proj = sb("bias_proj", [P, NPROJ])
        bias_scaled = sb("bias_scaled", [P, NPROJ])
        gamma_scaled = sb("gamma_scaled", [P, KB])
        state0_scaled = sb("state0_scaled", [P, KB])
        shared = sb("shared", [P, 2 * 2 * KB * L], U16)
        w_proj, beta_terms = (shared[:, i * 2 * NPROJ * D:(i + 1) * 2 * NPROJ * D].bitcast(F32)
                              .rearrange("p (j d) -> p j d", d=D) for i in range(2))
        w2_tern = shared[:, 4 * NPROJ * D:].bitcast(F16)
        out_halves = shared[:, 0:2 * KB * L].rearrange("p (h e l) -> p h e l", h=2, e=KB)
        out_words = shared[:, 0:2 * SUBS * D].bitcast(F32)
        turned_halves = shared[:, 2 * KB * L:].rearrange("p (h s e q) -> p h s e q", h=2, s=SUBS, e=KB)
        w_hi = sb("w_hi", [P, KB, NPROJ * P], F16)
        w_lo = sb("w_lo", [P, KB, NPROJ * P], F16)
        w1_rows = g_hi[:, 0:4, :].rearrange("p a b -> p (a b)").bitcast(F32)
        w1_tern = g_lo[:, 0:2, :].rearrange("p a b -> p (a b)")
        w1_below = g_lo[:, 2:4, :].rearrange("p a b -> p (a b)")
        w2_rows = state[:].rearrange("p a b -> p (a b)")
        w2_held = sb("w2_held", [P, SUBS * D])
        z_hi_rows, z_lo_rows = (zn[:, i * SUBS // 2:(i + 1) * SUBS // 2, :].rearrange("p s d -> p (s d)").bitcast(F16)
                                for i in range(2))
        x_hi_rows, x_lo_rows = (w2_held[:, i * L:(i + 1) * L].bitcast(F16) for i in range(2))
        magnitudes = gelu[:, 0:2, :].rearrange("p a b -> p (a b)")
        abs_sums = sb("abs_sums", [P, 2])
        threshold = sb("threshold", [P, 2])
        minus_threshold = sb("minus_threshold", [P, 2])
        w1T = sb("w1T", [P, KB, FF], F16)
        w2T = sb("w2T", [P, FB, D], F16)

        piece_loaded = [sem(f"piece_loaded{i}") for i in range(PIECES)]
        x_loaded = sem("x_loaded")
        gamma_loaded = sem("gamma_loaded")
        beta_loaded = sem("beta_loaded")
        par_loaded = sem("par_loaded")
        proj_loaded = sem("proj_loaded")
        w1_loaded = sem("w1_loaded")
        w2_loaded = sem("w2_loaded")
        out_stored = sem("out_stored")
        pool_consts = sem("pool_consts")
        ident_started = sem("ident_started")
        ident_made = sem("ident_made")
        ident16_made = sem("ident16_made")
        par_turned = sem("par_turned")
        par_ready = sem("par_ready")
        par_scaled = sem("par_scaled")
        proj_turned = sem("proj_turned")
        proj_hi = sem("proj_hi")
        proj_lo = sem("proj_lo")
        beta_applied = sem("beta_applied")
        beta_summed = sem("beta_summed")
        bias_summed = sem("bias_summed")
        bias_ready = sem("bias_ready")
        abs_summed = sem("abs_summed")
        mean_abs = sem("mean_abs")
        mean_floored = sem("mean_floored")
        threshold_ready = sem("threshold_ready")
        w1_compared = sem("w1_compared")
        ternary_ready = sem("ternary_ready")
        w2_held_done = sem("w2_held_done")
        w2_excess_done = sem("w2_excess_done")
        w2_ternary_ready = sem("w2_ternary_ready")
        w1_turned = sem("w1_turned")
        w1_placed = sem("w1_placed")
        w1_rest_placed = sem("w1_rest_placed")
        w2_turned = sem("w2_turned")
        bn_done = sem("bn_done")
        halves_done = sem("halves_done")
        moments_done = sem("moments_done")
        scalars_done = sem("scalars_done")
        xn_done = sem("xn_done")
        zn_done = sem("zn_done")
        zn_pool_done = sem("zn_pool_done")
        residual_done = sem("residual_done")
        z_turned = sem("z_turned")
        x_turned = sem("x_turned")
        z_hi_done = sem("z_hi_done")
        z_lo_done = sem("z_lo_done")
        x_hi_done = sem("x_hi_done")
        x_lo_done = sem("x_lo_done")
        z_hi_made = sem("z_hi_made")
        z_lo_made = sem("z_lo_made")
        x_hi_made = sem("x_hi_made")
        x_lo_made = sem("x_lo_made")
        z_hi_turned = sem("z_hi_turned")
        z_lo_turned = sem("z_lo_turned")
        x_hi_turned = sem("x_hi_turned")
        x_lo_turned = sem("x_lo_turned")
        gate_summed = sem("gate_summed")
        gate_done = sem("gate_done")
        in_summed = sem("in_summed")
        read_summed = sem("read_summed")
        decay_done = sem("decay_done")
        shifted_done = sem("shifted_done")
        inverse_done = sem("inverse_done")
        term_done = sem("term_done")
        sum_done = sem("sum_done")
        state_done = sem("state_done")
        read_done = sem("read_done")
        up_summed = sem("up_summed")
        gelu_done = sem("gelu_done")
        g_hi_done = sem("g_hi_done")
        g_lo_done = sem("g_lo_done")
        down_summed = sem("down_summed")
        last_summed = sem("last_summed")
        mixed_done = sem("mixed_done")
        halved0_done = sem("halved0_done")
        halved1_done = sem("halved1_done")
        halves_turned = sem("halves_turned")
        joined_done = sem("joined_done")
        out_turned = sem("out_turned")
        out_done = sem("out_done")
        last_done = sem("last_done")

        HALVES = ((0, SUBS // 2), (SUBS // 2, SUBS // 2))

        def last_sums(i, k):
            return slot[k][:, i % 2 * HALF:i % 2 * HALF + LAST_PIECES[i][1] * P]

        def last_rows(i):
            at, col = ((2, 0), (3, 0), (3, HALF))[i]
            return slot[at][:, col:col + LAST_PIECES[i][1] * D]

        def half_words(words, h):
            return words.bitcast(U16).rearrange("p (n h) -> p n h", h=2)[:, :, h]

        block = ctx.enter_context(nc.Block())

        def tile_rows(t, first, n):
            return rows[:, bass.ds(t * (SUBS * D) + first * D, n * D)]

        @block.sync
        def _(sp):
            n = SUBS // PIECES
            for i in range(PIECES):
                sp.dma_start(tile_rows(0, i * n, n).rearrange("p (s d) -> p s d", d=D),
                             x_rows[:, 0, i * n:(i + 1) * n, :]).then_inc(piece_loaded[i], 16)
            for i, w in enumerate((Wa, Wb, Wc)):
                sp.dma_start(w_proj[:, i * KB:(i + 1) * KB, :],
                             w.rearrange("(k p) d -> p k d", p=P)).then_inc(proj_loaded, 16)
            sp.dma_start(w1_rows.rearrange("p (f d) -> p f d", d=D),
                         W1.rearrange("(f p) d -> p f d", p=P)).then_inc(w1_loaded, 16)
            sp.dma_start(w2_rows.rearrange("p (k f) -> p k f", f=FF),
                         W2.rearrange("(k p) f -> p k f", p=P)).then_inc(w2_loaded, 16)
            for at, v in ((PROJ_BIAS, ba), (PROJ_BIAS + KB, bb), (PROJ_BIAS + 2 * KB, bc),
                          (STATE0, h0.rearrange("a d -> (a d)")), (B2, b2), (B1, b1)):
                n = v.shape[0] // P
                sp.dma_start(par_rows[at:at + n, :], v.rearrange("(k p) -> k p", p=P)).then_inc(par_loaded, 16)
            sp.wait_ge(w2_loaded, 16)
            for t in range(1, TILES):
                if t > 1:
                    sp.wait_ge(x_loaded, 16 * (t - 1))
                sp.dma_start(tile_rows(t, 0, SUBS).rearrange("p (s d) -> p s d", d=D),
                             x_rows[:, t]).then_inc(x_loaded, 16)

            def turn_halves(t):
                if t >= 1:
                    sp.wait_ge(joined_done, 2 * t)
                for e, made in enumerate((halved0_done, halved1_done)):
                    sp.wait_ge(made, 2 * t + 2)
                    for h in range(2):
                        sp.dma_start_transpose(turned_halves[:, h, :, e, :], out_halves[:, h, e, :]
                                               ).then_inc(halves_turned, 16)

            def store(t, pieces):
                for i, (s0, n) in enumerate(pieces):
                    if t < TILES - 1:
                        sp.wait_ge(out_done, t * 2 + i + 1)
                    else:
                        sp.wait_ge(last_done, i + 1)
                    sp.dma_start(out_rows[:, t, s0:s0 + n, :], tile_rows(t, s0, n).rearrange("p (s d) -> p s d", d=D)
                                 ).then_inc(out_stored, 16)

            def turn_parts(t):
                sp.wait_ge(read_summed, KB * t + KB)
                for src, dst, made, count, turned in (
                        (z_hi_rows, z_hi, z_hi_made, SUBS * t + SUBS, z_hi_turned),
                        (x_hi_rows, x_hi, x_hi_made, t + 1, x_hi_turned),
                        (z_lo_rows, z_lo, z_lo_made, SUBS * t + SUBS, z_lo_turned),
                        (x_lo_rows, x_lo, x_lo_made, t + 1, x_lo_turned)):
                    sp.wait_ge(made, count)
                    sp.dma_start_transpose(dst[:].rearrange("p s k q -> p (s k) q"), src).then_inc(turned, 16)

            for k in range(KB):
                sp.wait_ge(w2_ternary_ready, 1)
                sp.dma_start_transpose(w2T[:, :, k * P:(k + 1) * P], w2_tern[:, k * FF:(k + 1) * FF]
                                       ).then_inc(w2_turned, 16)
            for t in range(TILES):
                if t >= 1:
                    turn_halves(t - 1)
                if t < TILES - 1:
                    turn_parts(t)
                if t >= 1:
                    store(t - 1, HALVES)
            store(TILES - 1, LAST_PIECES)
            sp.wait_ge(out_stored, 16 * (2 * (TILES - 1) + len(LAST_PIECES)))

        @block.gpsimd
        def _(pool):
            nc.gpsimd.memset(ident[:], 0.0).then_inc(ident_started, 1)
            pool.wait_ge(ident_started, 1)
            nc.gpsimd.affine_select(out=ident[:], in_=ident[:], compare_op=ALU.not_equal, fill=1.0,
                                    base=0, pattern=[[-1, P]], channel_multiplier=1).then_inc(ident_made, 1)
            nc.gpsimd.memset(minus_half[:], -0.5).then_inc(pool_consts, 1)
            nc.gpsimd.memset(row_scale[:], ROW_SCALE).then_inc(pool_consts, 1)
            nc.gpsimd.memset(averager[:], 1.0 / (FF * D)).then_inc(pool_consts, 1)
            nc.gpsimd.memset(zeros[:], 0.0).then_inc(pool_consts, 1)

            def norm_scalars(g, s0=0, s1=SUBS):
                n = 5 * g
                c = slice(s0, s1)
                pool.wait_ge(moments_done, 4 * g + 4)
                nc.gpsimd.tensor_tensor(rstd[:, c], var_eps[:, c], minus_half[:, c], ALU.pow).then_inc(scalars_done, 1)
                nc.gpsimd.tensor_tensor(rstd_both[:, c], both_eps[:, c], minus_half[:, c],
                                        ALU.pow).then_inc(scalars_done, 1)
                pool.wait_ge(scalars_done, n + 2)
                nc.gpsimd.tensor_tensor(std[:, c], var_eps[:, c], rstd[:, c], ALU.mult).then_inc(scalars_done, 1)
                nc.gpsimd.tensor_tensor(rstd_both[:, c], rstd_both[:, c], row_scale[:, c],
                                        ALU.mult).then_inc(scalars_done, 1)
                pool.wait_ge(scalars_done, n + 4)
                nc.gpsimd.tensor_tensor(rstd_n[:, c], rstd_both[:, c], std[:, c], ALU.mult).then_inc(scalars_done, 1)

            def residuals(t):
                for half in range(2):
                    n = SUBS // 2
                    pool.wait_ge(xn_done, SUBS * t + n * (half + 1))
                    r = tile_rows(t, half * n, n)
                    nc.gpsimd.tensor_tensor(r, r, xn[:, half * n:(half + 1) * n, :].rearrange("p s d -> p (s d)"),
                                            ALU.add).then_inc(residual_done, 1)

            def finish_rows(t):
                for half, (s0, n) in enumerate(HALVES):
                    r = tile_rows(t, s0, n)
                    pool.wait_ge(joined_done, 2 * t + 2)
                    pool.wait_ge(residual_done, 2 * t + half + 1)
                    nc.gpsimd.tensor_tensor(r, r, out_words[:, s0 * D:(s0 + n) * D], ALU.add).then_inc(out_done, 1)

            def tile(t, first, last):
                for f in range(FB):
                    if f == G_BUFFERS and not last:
                        norm_scalars(t + 2)
                    pool.wait_ge(g_hi_done, FB * t + f + 1)
                    nc.gpsimd.tensor_tensor(g_lo[:, f, :], gelu[:, f % G_BUFFERS, :], g_hi[:, f, :],
                                            ALU.subtract).then_inc(g_lo_done, 1)
                if not last:
                    residuals(t + 1)
                if not first:
                    finish_rows(t - 1)

            pool.wait_ge(pool_consts, 2)
            norm_scalars(0, 0, SUBS // 2)
            norm_scalars(1, SUBS // 2, SUBS)
            pool.wait_ge(scalars_done, 10)
            for s in range(SUBS - ZN_POOL, SUBS):
                pool.wait_ge(xn_done, s + 1)
                nc.gpsimd.tensor_scalar(zn[:, s, :], xn[:, s, :], rstd_n[:, s:s + 1], 1.0,
                                        ALU.mult, ALU.mult).then_inc(zn_pool_done, 1)
            pool.wait_ge(beta_loaded, 16)
            pool.wait_ge(proj_loaded, 16 * 3)
            nc.gpsimd.tensor_tensor(beta_terms, w_proj, beta_rows[:].unsqueeze(1).broadcast_to([P, NPROJ, D]),
                                    ALU.mult).then_inc(beta_applied, 1)
            residuals(0)
            pool.wait_ge(threshold_ready, 2)
            nc.gpsimd.tensor_scalar(w2_held[:], w2_rows, threshold[:, 1:2], minus_threshold[:, 1:2],
                                    ALU.min, ALU.max).then_inc(w2_held_done, 1)
            pool.wait_ge(w2_held_done, 1)
            nc.gpsimd.tensor_tensor(w2_held[:], w2_rows, w2_held[:], ALU.subtract).then_inc(w2_excess_done, 1)
            tile(0, True, False)
            with pool.Fori(1, TILES - 1) as t:
                tile(t, False, False)
            tile(TILES - 1, False, True)

        @block.scalar
        def _(act):
            act.dma_start(gamma_rows[:], gamma.rearrange("(k p) -> k p", p=P)).then_inc(gamma_loaded, 16)
            act.dma_start(beta_rows[:], beta.rearrange("(a d) -> a d", a=1).broadcast_to([P, D])
                          ).then_inc(beta_loaded, 16)
            act.wait_ge(ident_made, 1)
            nc.scalar.copy(ident16[:], ident[:]).then_inc(ident16_made, 1)

            def high_part(k, turned, hi, done, at, scale):
                act.wait_ge(turned, k + 1)
                nc.scalar.activation(hi[:, :, k, :], slot[at + k][:].rearrange("p (s q) -> p s q", q=P), ACT.Copy,
                                     scale=scale).then_inc(done, 1)

            act.wait_ge(scalars_done, 5)
            for s in range(SUBS - ZN_POOL):
                act.wait_ge(xn_done, s + 1)
                nc.scalar.mul(zn[:, s, :], xn[:, s, :], rstd_n[:, s:s + 1]).then_inc(zn_done, 1)
            act.wait_ge(par_scaled, 1)
            for k in range(KB):
                act.wait_ge(proj_turned, k + 1)
                nc.scalar.activation(w_hi[:, k, :], slot[k][:, 0:NPROJ * P], ACT.Copy,
                                     scale=gamma_scaled[:, k:k + 1]).then_inc(proj_hi, 1)

            def magnitude_sums(m, w, loaded):
                act.wait_ge(loaded, 16)
                if m:
                    act.wait_ge(abs_summed, m)
                nc.scalar.activation(magnitudes, w, ACT.Abs, accum_out=abs_sums[:, m:m + 1]).then_inc(abs_summed, 1)

            magnitude_sums(0, w1_rows, w1_loaded)
            for k in range(KB):
                high_part(k, x_turned, x_hi, x_hi_done, 2, ROW_SCALE)
            for k in range(KB):
                high_part(k, z_turned, z_hi, z_hi_done, 0, 1.0)
            magnitude_sums(1, w2_rows, w2_loaded)
            act.wait_ge(beta_applied, 1)
            for j in range(NPROJ):
                if j >= 2:
                    act.wait_ge(beta_summed, j - 1)
                nc.scalar.activation(beta_copy[:, j % 2, :], beta_terms[:, j, :], ACT.Copy,
                                     accum_out=beta_sums[:, j:j + 1]).then_inc(beta_summed, 1)

            def tile(t, first, last):
                for e in range(KB):
                    if first and e == 1:
                        act.wait_ge(w1_turned, 1)
                        nc.scalar.copy(w1T[:, 0, :], slot[0][:, 0:HALF].bitcast(F16)).then_inc(w1_placed, 1)
                    act.wait_ge(gate_summed, KB * t + e + 1)
                    nc.scalar.activation(decay[:, e, :], slot[2 + e][:], ACT.Sigmoid, bias=bias_proj[:, e:e + 1],
                                         scale=1.0 / PROJ_SCALE).then_inc(gate_done, 1)

                def g_high(f):
                    act.wait_ge(gelu_done, FB * t + f + 1)
                    nc.scalar.copy(g_hi[:, f, :], gelu[:, f % G_BUFFERS, :]).then_inc(g_hi_done, 1)

                for f in range(FB):
                    act.wait_ge(up_summed, FB * t + f + 1)
                    if f >= G_BUFFERS:
                        act.wait_ge(g_lo_done, FB * t + f - G_BUFFERS + 1)
                    nc.scalar.activation(gelu[:, f % G_BUFFERS, :], slot[f % 4][:], ACT.Gelu,
                                         bias=par[:, B1 + f:B1 + f + 1], scale=1.0 / ROW_SCALE).then_inc(gelu_done, 1)
                    if f >= 1:
                        g_high(f - 1)
                    if first and f == FB - 2:
                        act.wait_ge(w2_excess_done, 1)
                        nc.scalar.activation(w2_tern, w2_held[:], ACT.Sign).then_inc(w2_ternary_ready, 1)
                g_high(FB - 1)
                if not last:
                    act.wait_ge(scalars_done, 5 * t + 15)
                    for s in range(SUBS):
                        act.wait_ge(xn_done, SUBS * t + SUBS + s + 1)
                        nc.scalar.mul(z_hi_rows[:, s * D:(s + 1) * D], xn[:, s, :], rstd_n[:, s:s + 1]
                                      ).then_inc(z_hi_made, 1)
                    if first:
                        act.wait_ge(w2_ternary_ready, 1)
                    nc.scalar.activation(x_hi_rows, xn[:].rearrange("p s d -> p (s d)"), ACT.Copy,
                                         scale=ROW_SCALE).then_inc(x_hi_made, 1)
                if not first:
                    act.wait_ge(halves_turned, 64 * t)
                    for h in range(2):
                        nc.scalar.copy(half_words(out_words, h),
                                       turned_halves[:, h].rearrange("p s e q -> p (s e q)")
                                       ).then_inc(joined_done, 1)
                if not last:
                    if not first:
                        act.wait_ge(out_done, 2 * t)
                    act.wait_ge(mixed_done, KB * t + 1)
                    for h in range(2):
                        nc.scalar.copy(out_halves[:, h, 0, :], half_words(state[:, 0, :], h)
                                       ).then_inc(halved0_done, 1)

            act.wait_ge(bias_ready, 1)
            tile(0, True, False)
            with act.Fori(1, TILES - 1) as t:
                tile(t, False, False)
            tile(TILES - 1, False, True)

        @block.tensor
        def _(pe):
            def turn_norm(k, src, turned, at):
                for s in range(SUBS):
                    mm = nc.tensor.transpose(slot[at + k][:, s * P:(s + 1) * P], src[:, s, k * P:(k + 1) * P], ident[:])
                mm.then_inc(turned, 1)

            def half_subs(half):
                return slice(half * SUBS // 2, (half + 1) * SUBS // 2)

            def project(dst, j, summed, low=None):
                passes = [(w, z, k) for w, z in ((w_hi, z_hi), (w_lo, z_hi), (w_hi, z_lo)) for k in range(KB)]
                for n, (w, z, k) in enumerate(passes):
                    if low is not None and n == 2 * KB:
                        pe.wait_ge(*low)
                    for half in range(2):
                        c = slice(half * HALF, (half + 1) * HALF)
                        mm = nc.tensor.matmul(dst[:, c], w[:, k, j * P:(j + 1) * P], z[:, half_subs(half), k, :],
                                              start=(n == 0), stop=(n == len(passes) - 1))
                mm.then_inc(summed, 1)

            pe.wait_ge(ident_made, 1)
            pe.wait_ge(gamma_loaded, 16)
            nc.tensor.transpose(slot[2][:, 0:KB], gamma_rows[:], ident[0:KB, 0:KB]).then_inc(par_turned, 1)
            pe.wait_ge(proj_loaded, 16 * 3)
            for k in range(KB):
                for j in range(NPROJ):
                    mm = nc.tensor.transpose(slot[k][:, j * P:(j + 1) * P], w_proj[:, j, k * P:(k + 1) * P], ident[:])
                mm.then_inc(proj_turned, 1)

            def average_magnitude(m, at):
                pe.wait_ge(abs_summed, m + 1)
                nc.tensor.matmul(slot[at][:, 0:1], averager[:], abs_sums[:, m:m + 1],
                                 start=True, stop=True).then_inc(mean_abs, 1)

            def turn_w1():
                pe.wait_ge(ident16_made, 1)
                pe.wait_ge(ternary_ready, 1)
                turned = slot[0][:].bitcast(F16)
                for k in range(KB):
                    for f in range(FB):
                        mm = nc.tensor.transpose(turned[:, k * FF + f * P:k * FF + (f + 1) * P],
                                                 w1_tern[:, f * D + k * P:f * D + (k + 1) * P], ident16[:])
                mm.then_inc(w1_turned, 1)

            pe.wait_ge(par_scaled, 1)
            pe.wait_ge(xn_done, SUBS)
            turn_norm(0, xn, x_turned, 2)
            turn_norm(1, xn, x_turned, 2)
            pe.wait_ge(pool_consts, 3)
            pe.wait_ge(proj_lo, 2)
            average_magnitude(0, 1)
            pe.wait_ge(zn_pool_done, ZN_POOL)
            pe.wait_ge(zn_done, SUBS - ZN_POOL)
            turn_norm(0, zn, z_turned, 0)
            pe.wait_ge(mean_floored, 1)
            turn_norm(1, zn, z_turned, 0)

            def turn_small():
                pe.wait_ge(z_lo_done, KB)
                pe.wait_ge(par_loaded, 16 * 6)
                nc.tensor.transpose(slot[1][:, HALF:HALF + NPAR], par_rows[:], ident[0:NPAR, 0:NPAR]
                                    ).then_inc(par_turned, 1)
                average_magnitude(1, 1)

            def turn_out(s0, n, mixed, dst):
                pe.wait_ge(mixed_done, mixed)
                for s in range(n):
                    for e in range(KB):
                        mm = nc.tensor.transpose(dst[:, s * D + e * P:s * D + (e + 1) * P],
                                                 state[:, e, (s0 + s) * P:(s0 + s + 1) * P], ident[:])
                mm.then_inc(out_turned, 1)

            def down(t, k, parts, summed):
                for f in range(FB):
                    pe.wait_ge(g_lo_done, FB * t + f + 1)
                    for g in (g_hi, g_lo):
                        for dst, c in parts:
                            mm = nc.tensor.matmul(dst, w2T[:, f, k * P:(k + 1) * P], g[:, f, c],
                                                  start=(f == 0 and g is g_hi), stop=(f == FB - 1 and g is g_lo))
                mm.then_inc(summed, 1)

            def in_halves(dst):
                return [(dst[:, c], c) for c in (slice(0, HALF), slice(HALF, L))]

            def tile(t, first, last):
                for e in range(KB):
                    if first:
                        pe.wait_ge(z_hi_done, KB)
                        pe.wait_ge(x_lo_done, e + 1)
                        project(slot[2 + e], e, gate_summed, low=(z_lo_done, KB))
                    else:
                        pe.wait_ge(z_hi_turned, 16 * t)
                        pe.wait_ge((term_done, read_done)[e], KB * t)
                        project(slot[2 + e], e, gate_summed, low=(z_lo_turned, 16 * t))
                    if first and e == 0:
                        turn_small()
                if first:
                    turn_w1()
                for f in range(FB):
                    if f < 2:
                        if first:
                            pe.wait_ge(w1_placed, 1)
                            pe.wait_ge(w1_rest_placed, 1)
                            pe.wait_ge(par_ready, 1)
                            pe.wait_ge(mean_floored, 2)
                        else:
                            pe.wait_ge(x_hi_turned, 16 * t)
                            pe.wait_ge(x_lo_turned, 16 * t)
                            pe.wait_ge(mixed_done, KB * t - KB + f + 1)
                    elif f < 4:
                        pe.wait_ge(gate_done, KB * t + f - 2 + 1)
                    else:
                        pe.wait_ge(gelu_done, FB * t + f - 4 + 1)
                    dst = slot[f % 4]
                    for k in range(KB):
                        for n, xs in enumerate((x_hi, x_lo)):
                            for half in range(2):
                                c = slice(half * HALF, (half + 1) * HALF)
                                mm = nc.tensor.matmul(dst[:, c], w1T[:, k, f * P:(f + 1) * P], xs[:, half_subs(half), k, :],
                                                      start=(k == 0 and n == 0), stop=(k == KB - 1 and n == 1))
                    mm.then_inc(up_summed, 1)
                for i, (j, summed) in enumerate(((KB, in_summed), (2 * KB, read_summed),
                                                 (KB + 1, in_summed), (2 * KB + 1, read_summed))):
                    pe.wait_ge(gelu_done, FB * t + 5 + i)
                    project(slot[i], j, summed)
                if not last:
                    if first:
                        pe.wait_ge(w2_turned, 16 * KB)
                    pe.wait_ge(term_done, KB * t + 1)
                    down(t, 0, in_halves(slot[0]), down_summed)
                    pe.wait_ge(read_done, KB * t + 1)
                    down(t, 1, in_halves(slot[1]), down_summed)

            tile(0, True, False)
            with pe.Fori(1, TILES - 1) as t:
                tile(t, False, False)
            t = TILES - 1
            tile(t, False, True)

            def turn_piece(i):
                turn_out(*LAST_PIECES[i], KB * t + KB * (i + 1), last_rows(i))

            for i, (s0, n) in enumerate(LAST_PIECES):
                for k in range(KB):
                    if i == 0:
                        pe.wait_ge((term_done, read_done)[k], KB * t + 1)
                    down(t, k, [(last_sums(i, k), slice(s0 * P, (s0 + n) * P))], last_summed)
                    if i >= 1 and k == 0:
                        turn_piece(i - 1)
            turn_piece(len(LAST_PIECES) - 1)

        @block.vector
        def _(dve):
            def statistics(t):
                dve.wait_ge(x_loaded, 16 * t)
                for s in range(SUBS):
                    nc.vector.bn_stats(bn[:, s, :], tile_rows(t, s, 1)).then_inc(bn_done, 1)

            ALL = slice(0, SUBS)

            def sums(g, c=ALL):
                dve.wait_ge(bn_done, SUBS * g if c == ALL else c.stop)
                nc.vector.tensor_tensor(mean_gap[:, c], bn[:, c, 1], bn[:, c, 4], ALU.subtract).then_inc(halves_done, 1)
                nc.vector.tensor_tensor(mean_sum[:, c], bn[:, c, 1], bn[:, c, 4], ALU.add).then_inc(halves_done, 1)
                nc.vector.tensor_tensor(square_sum[:, c], bn[:, c, 2], bn[:, c, 5], ALU.add).then_inc(halves_done, 1)

            def means(g, c=ALL):
                dve.wait_ge(halves_done, 4 * g + 1)
                nc.vector.scalar_tensor_tensor(gap_square[:, c], mean_gap[:, c], 0.25, mean_gap[:, c],
                                               ALU.mult, ALU.mult).then_inc(halves_done, 1)
                dve.wait_ge(halves_done, 4 * g + 2)
                nc.vector.tensor_scalar(mean[:, c], mean_sum[:, c], 0.5, None, ALU.mult).then_inc(moments_done, 1)

            def variances(g, c=ALL):
                dve.wait_ge(halves_done, 4 * g + 4)
                nc.vector.scalar_tensor_tensor(var[:, c], square_sum[:, c], 1.0 / D, gap_square[:, c],
                                               ALU.mult, ALU.add).then_inc(moments_done, 1)

            def variances_eps(g, c=ALL):
                dve.wait_ge(moments_done, 4 * g + 2)
                nc.vector.tensor_scalar(var_eps[:, c], var[:, c], LN_EPS, None, ALU.add).then_inc(moments_done, 1)

            def variances_both_eps(g, c=ALL):
                dve.wait_ge(moments_done, 4 * g + 3)
                nc.vector.scalar_tensor_tensor(both_eps[:, c], var_eps[:, c], LN_EPS, var[:, c],
                                               ALU.mult, ALU.add).then_inc(moments_done, 1)

            def first_norm(g, t, s0=0, s1=SUBS):
                dve.wait_ge(scalars_done, 5 * g + 1)
                for s in range(s0, s1):
                    nc.vector.tensor_scalar(xn[:, s, :], tile_rows(t, s, 1), mean[:, s:s + 1], rstd[:, s:s + 1],
                                            ALU.subtract, ALU.mult).then_inc(xn_done, 1)

            def low_part(k, hi_done, hi, lo, done, at, scale):
                dve.wait_ge(hi_done, k + 1)
                nc.vector.scalar_tensor_tensor(lo[:, :, k, :], slot[at + k][:].rearrange("p (s q) -> p s q", q=P),
                                               scale, hi[:, :, k, :], ALU.mult, ALU.subtract).then_inc(done, 1)

            for g in range(2):
                for s in range(g * SUBS // 2, (g + 1) * SUBS // 2):
                    if s % (SUBS // PIECES) == 0:
                        dve.wait_ge(piece_loaded[s // (SUBS // PIECES)], 16)
                    nc.vector.bn_stats(bn[:, s, :], tile_rows(0, s, 1)).then_inc(bn_done, 1)
                for step in (sums, means, variances, variances_eps, variances_both_eps):
                    step(g, slice(g * SUBS // 2, (g + 1) * SUBS // 2))
            dve.wait_ge(par_turned, 1)
            nc.vector.tensor_scalar(gamma_scaled[:], slot[2][:, 0:KB], WEIGHT_SCALE, None,
                                    ALU.mult).then_inc(par_scaled, 1)
            first_norm(0, 0, 0, SUBS // 2)
            first_norm(1, 0, SUBS // 2, SUBS)
            for k in range(KB):
                dve.wait_ge(proj_hi, k + 1)
                nc.vector.scalar_tensor_tensor(w_lo[:, k, :], slot[k][:, 0:NPROJ * P], gamma_scaled[:, k:k + 1],
                                               w_hi[:, k, :], ALU.mult, ALU.subtract).then_inc(proj_lo, 1)
            def thresholds(m, at):
                dve.wait_ge(mean_abs, m + 1)
                nc.vector.tensor_scalar(threshold[:, m:m + 1], slot[at][:, 0:1], TERNARY_EPS, 0.5,
                                        ALU.max, ALU.mult).then_inc(mean_floored, 1)
                dve.wait_ge(mean_floored, m + 1)
                nc.vector.tensor_scalar(minus_threshold[:, m:m + 1], threshold[:, m:m + 1], -1.0, None,
                                        ALU.mult).then_inc(threshold_ready, 1)

            thresholds(0, 1)
            for k in range(KB):
                low_part(k, x_hi_done, x_hi, x_lo, x_lo_done, 2, ROW_SCALE)
            for k in range(KB):
                low_part(k, z_hi_done, z_hi, z_lo, z_lo_done, 0, 1.0)
            dve.wait_ge(threshold_ready, 1)
            nc.vector.tensor_scalar(w1_below, w1_rows, minus_threshold[:, 0:1], None,
                                    ALU.is_lt).then_inc(w1_compared, 1)
            dve.wait_ge(par_turned, 2)
            nc.vector.tensor_copy(par[:], slot[1][:, HALF:HALF + NPAR]).then_inc(par_ready, 1)
            thresholds(1, 1)
            dve.wait_ge(w1_compared, 1)
            nc.vector.scalar_tensor_tensor(w1_tern, w1_rows, threshold[:, 0:1], w1_below,
                                           ALU.is_gt, ALU.subtract).then_inc(ternary_ready, 1)
            dve.wait_ge(beta_summed, NPROJ)
            dve.wait_ge(par_ready, 1)
            nc.vector.tensor_tensor(bias_proj[:], beta_sums[:], par[:, PROJ_BIAS:PROJ_BIAS + NPROJ],
                                    ALU.add).then_inc(bias_summed, 1)
            nc.vector.tensor_scalar(state0_scaled[:], par[:, STATE0:STATE0 + KB], 1.0 / PROJ_SCALE, None,
                                    ALU.mult).then_inc(par_scaled, 1)
            dve.wait_ge(bias_summed, 1)
            nc.vector.tensor_scalar(bias_scaled[:], bias_proj[:], PROJ_SCALE, None, ALU.mult).then_inc(bias_ready, 1)
            dve.wait_ge(pool_consts, 4)

            def decay_product(t, e):
                dve.wait_ge(gate_done, KB * t + e + 1)
                nc.vector.tensor_tensor_scan(decay[:, e, :], decay[:, e, :], zeros[:], 1.0,
                                             ALU.mult, ALU.add).then_inc(decay_done, 1)

            def shift_decay(t, e):
                dve.wait_ge(decay_done, KB * t + e + 1)
                nc.vector.tensor_scalar(inverse[:, e, :], decay[:, e, :], SCAN_EPS, PROJ_SCALE * PROJ_SCALE,
                                        ALU.add, ALU.mult).then_inc(shifted_done, 1)

            def invert_decay(t, e):
                dve.wait_ge(shifted_done, KB * t + e + 1)
                nc.vector.reciprocal(inverse[:, e, :], inverse[:, e, :]).then_inc(inverse_done, 1)

            dve.wait_ge(w1_turned, 1)
            nc.vector.tensor_copy(w1T[:, 1, :], slot[0][:, HALF:L].bitcast(F16)).then_inc(w1_rest_placed, 1)
            decay_product(0, 0)

            def finish_rows(t, i):
                dve.wait_ge(out_turned, i + 1)
                r = tile_rows(t, *LAST_PIECES[i])
                nc.vector.tensor_tensor(r, last_rows(i), r, ALU.add).then_inc(last_done, 1)

            def tile(t, first, last):
                if not last and not first:
                    statistics(t + 1)
                n = KB * t
                in_slot, read_slot = (0, 2), (1, 3)
                if not first:
                    decay_product(t, 0)
                    if not last:
                        sums(t + 2)
                shift_decay(t, 0)
                if not last and not first:
                    means(t + 2)
                invert_decay(t, 0)
                if first:
                    statistics(1)
                    sums(2)
                    means(2)
                if not last:
                    variances(t + 2)
                decay_product(t, 1)
                if not last:
                    variances_eps(t + 2)
                shift_decay(t, 1)
                if not last:
                    variances_both_eps(t + 2)
                invert_decay(t, 1)
                if not first:
                    dve.wait_ge(halved0_done, 2 * t)
                for e in range(KB):
                    dve.wait_ge(inverse_done, n + e + 1)
                    dve.wait_ge(in_summed, n + e + 1)
                    nc.vector.scalar_tensor_tensor(state[:, e, :], slot[in_slot[e]][:],
                                                   bias_scaled[:, KB + e:KB + e + 1], inverse[:, e, :],
                                                   ALU.add, ALU.mult).then_inc(term_done, 1)
                    dve.wait_ge(term_done, n + e + 1)
                    nc.vector.tensor_tensor_scan(state[:, e, :], state[:, e, :], zeros[:], 0.0,
                                                 ALU.add, ALU.add).then_inc(sum_done, 1)
                    dve.wait_ge(sum_done, n + e + 1)
                    nc.vector.scalar_tensor_tensor(state[:, e, :], state[:, e, :], state0_scaled[:, e:e + 1],
                                                   decay[:, e, :], ALU.add, ALU.mult).then_inc(state_done, 1)
                    dve.wait_ge(state_done, n + e + 1)
                    dve.wait_ge(read_summed, n + e + 1)
                    nc.vector.scalar_tensor_tensor(state[:, e, :], slot[read_slot[e]][:],
                                                   bias_scaled[:, 2 * KB + e:2 * KB + e + 1], state[:, e, :],
                                                   ALU.add, ALU.mult).then_inc(read_done, 1)
                    if e == 0 and not last:
                        dve.wait_ge(residual_done, 2 * t + 2)
                        first_norm(t + 2, t + 1)
                if not last:
                    for s in range(SUBS):
                        dve.wait_ge(z_hi_made, SUBS * t + s + 1)
                        nc.vector.scalar_tensor_tensor(z_lo_rows[:, s * D:(s + 1) * D], xn[:, s, :], rstd_n[:, s:s + 1],
                                                       z_hi_rows[:, s * D:(s + 1) * D], ALU.mult, ALU.subtract
                                                       ).then_inc(z_lo_made, 1)
                    dve.wait_ge(read_done, n + KB)
                    mix(0, slot[0][:], slice(0, L), down_summed, n + 1)
                    dve.wait_ge(x_hi_made, t + 1)
                    nc.vector.scalar_tensor_tensor(x_lo_rows, xn[:].rearrange("p s d -> p (s d)"), ROW_SCALE,
                                                   x_hi_rows, ALU.mult, ALU.subtract).then_inc(x_lo_made, 1)
                    mix(1, slot[1][:], slice(0, L), down_summed, n + 2)
                    if not first:
                        dve.wait_ge(out_done, 2 * t)
                    dve.wait_ge(mixed_done, n + 2)
                    for h in range(2):
                        nc.vector.tensor_copy(out_halves[:, h, 1, :], half_words(state[:, 1, :], h)
                                              ).then_inc(halved1_done, 1)

            def mix(e, src, c, summed, count):
                dve.wait_ge(summed, count)
                nc.vector.scalar_tensor_tensor(state[:, e, c], src, par[:, B2 + e:B2 + e + 1],
                                               state[:, e, c], ALU.add, ALU.add).then_inc(mixed_done, 1)

            tile(0, True, False)
            with dve.Fori(1, TILES - 1) as t:
                tile(t, False, False)
            t = TILES - 1
            tile(t, False, True)
            dve.wait_ge(read_done, KB * t + KB)
            for i, (s0, n) in enumerate(LAST_PIECES):
                for e in range(KB):
                    mix(e, last_sums(i, e), slice(s0 * P, (s0 + n) * P), last_summed, KB * i + e + 1)
                    if i >= 1 and e == 0:
                        finish_rows(t, i - 1)
            i = len(LAST_PIECES) - 1
            finish_rows(t, i)


_INS = ["L0_attn_X", "L0_attn_Wa", "L0_attn_ba", "L0_attn_Wb", "L0_attn_bb", "L0_attn_Wc", "L0_attn_bc",
        "L0_attn_gamma", "L0_attn_beta", "L0_attn_h0", "L0_ffn_W1", "L0_ffn_b1", "L0_ffn_W2", "L0_ffn_b2"]


def kernel(**inputs):
    import numpy as _np
    import concourse.bacc as _bacc
    from concourse import mybir as _mybir
    from concourse.bass_utils import run_bass_kernel_spmd as _run

    nc = _bacc.Bacc("TRN2", target_bir_lowering=False, num_devices=1)
    arrays, args = {}, []
    for name in _INS:
        a = _np.ascontiguousarray(inputs[name])
        arrays[f"in_{name}_dram"] = a
        args.append(nc.dram_tensor(f"in_{name}_dram", a.shape, _mybir.dt.from_np(a.dtype), kind="ExternalInput").ap())
    shape = inputs["L0_attn_X"].shape
    args.append(nc.dram_tensor("out_dram", shape, _mybir.dt.float32, kind="ExternalOutput").ap())
    build(nc, *args)
    r = _run(nc, [arrays], core_ids=[0])
    return r.results[0]["out_dram"]
```
